# Optimizing a Trainium2 kernel written in Bass

```python
import numpy as np
import jax
import jax.numpy as jnp

def _softmax(x, axis=-1):
    return jax.nn.softmax(x, axis=axis)

def _gelu(x):
    return jax.nn.gelu(x, approximate=True)

def _silu(x):
    return jax.nn.silu(x)

def _sigmoid(x):
    return jax.nn.sigmoid(x)

def _layernorm(x, axis=-1, eps=1e-05):
    m = jnp.mean(x, axis=axis, keepdims=True)
    v = jnp.var(x, axis=axis, keepdims=True)
    return (x - m) / jnp.sqrt(v + eps)

def _scatter_add(tgt, idx, src, axis=0):
    return tgt.at[idx].add(src)

def _segment_sum(src, seg, n):
    return jax.ops.segment_sum(src, seg, n)
kernel_name = 'mk_adaln_ffn_d2_seqx_r8_36c87a'

def setup_inputs(seed: int=0):
    np.random.seed(seed)
    _w = jnp.asarray

    def _rec_inputs():
        import jax
        import jax.numpy as jnp
        _rk = jax.random.key(seed)
        x = -7.109e-05 + 0.9999 * jax.random.normal(jax.random.fold_in(_rk, 1), (128, 32, 256), jnp.float32)
        _lenS = 32 - jax.random.randint(jax.random.fold_in(_rk, 7), (128,), 0, max(1, 32 // 4) + 1, jnp.int32)
        _lenS2 = 32 - jax.random.randint(jax.random.fold_in(_rk, 8), (128,), 0, max(1, 32 // 4) + 1, jnp.int32)
        itok_B_0_7 = jax.random.randint(jax.random.fold_in(_rk, 11), (128,), 0, 8, jnp.int32)
        return (x, itok_B_0_7)
    x, itok_B_0_7 = _rec_inputs()

    def _L0_cond_setup():
        import jax, jax.numpy as jnp
        import numpy as np
        B, C, D, T, N_SUBJECTS = (128, 32, 32, 256, 8)
        key = jax.random.key(seed)
        kx, ks, kw = jax.random.split(key, 3)
        x = jax.random.normal(kx, (B, C, T), dtype=jnp.float32)
        subjects = jax.random.randint(ks, (B,), 0, N_SUBJECTS, dtype=jnp.int64)
        weights = jax.random.normal(kw, (N_SUBJECTS, C, D), dtype=jnp.float32) * (1.0 / C ** 0.5)
        return {'x': x, 'subjects': subjects, 'weights': weights}
    _L0_cond_all = _L0_cond_setup()
    _L0_cond_in = {k: v for k, v in _L0_cond_all.items() if k in ('weights',)}
    del _L0_cond_all

    def _L0_ffn_setup():
        import jax, jax.numpy as jnp
        import numpy as np
        B, T, D, E, H = (4, 256, 256, 4, 1024)
        TOPK = 2
        CAPACITY_FACTOR = 1
        key = jax.random.key(seed)
        k0, k1, k2, k3 = jax.random.split(key, 4)
        x = jax.random.normal(k0, (B, T, D), dtype=jnp.float32)
        Wg = jax.random.normal(k1, (D, E), dtype=jnp.float32) * 0.02
        bg = jnp.zeros((E,), dtype=jnp.float32)
        W1 = jax.random.normal(k2, (E, D, H), dtype=jnp.float32) * (1.0 / np.sqrt(D))
        W2 = jax.random.normal(k3, (E, H, D), dtype=jnp.float32) * (1.0 / np.sqrt(H))
        return {'x': x, 'Wg': Wg, 'bg': bg, 'W1': W1, 'W2': W2}
    _L0_ffn_all = _L0_ffn_setup()
    _L0_ffn_in = {k: v for k, v in _L0_ffn_all.items() if k in ('Wg', 'bg', 'W1', 'W2')}
    del _L0_ffn_all

    def _L1_cond_setup():
        import jax, jax.numpy as jnp
        import numpy as np

        def _lora_linear(x, W, A, B, adapter_indices):
            base = jnp.einsum('bsd,df->bsf', x, W)
            Ai = A[adapter_indices]
            Bi = B[adapter_indices]
            lora = jnp.einsum('bsr,brf->bsf', jnp.einsum('bsd,bdr->bsr', x, Ai), Bi)
            return base + lora
        key = jax.random.key(seed)
        ks = jax.random.split(key, 10)
        H, I, N, R = (256, 1024, 8, 16)
        B, S = (4, 256)
        std_h = 1.0 / np.sqrt(H)
        std_i = 1.0 / np.sqrt(I)
        x = jax.random.normal(ks[0], (B, S, H), dtype=jnp.float32)
        adapter_indices = jax.random.randint(ks[1], (B,), 0, N, dtype=jnp.int32)
        Wg = jax.random.normal(ks[2], (H, I), dtype=jnp.float32) * std_h
        Wu = jax.random.normal(ks[3], (H, I), dtype=jnp.float32) * std_h
        Wd = jax.random.normal(ks[4], (I, H), dtype=jnp.float32) * std_i
        Ag = jax.random.normal(ks[5], (N, H, R), dtype=jnp.float32) * std_h
        Bg = jnp.zeros((N, R, I), dtype=jnp.float32) + 0.01
        Au = jax.random.normal(ks[6], (N, H, R), dtype=jnp.float32) * std_h
        Bu = jnp.zeros((N, R, I), dtype=jnp.float32) + 0.01
        Ad = jax.random.normal(ks[7], (N, I, R), dtype=jnp.float32) * std_i
        Bd = jnp.zeros((N, R, H), dtype=jnp.float32) + 0.01
        return {'x': x, 'Wg': Wg, 'Wu': Wu, 'Wd': Wd, 'Ag': Ag, 'Bg': Bg, 'Au': Au, 'Bu': Bu, 'Ad': Ad, 'Bd': Bd, 'adapter_indices': adapter_indices}
    _L1_cond_all = _L1_cond_setup()
    _L1_cond_in = {k: v for k, v in _L1_cond_all.items() if k in ('Wg', 'Wu', 'Wd', 'Ag', 'Bg', 'Au', 'Bu', 'Ad', 'Bd')}
    del _L1_cond_all

    def _L1_ffn_setup():
        import jax, jax.numpy as jnp
        import numpy as np
        key = jax.random.key(seed)
        k1, k2, k3, k4 = jax.random.split(key, 4)
        B, S, D_IN, D_OUT = (4, 512, 256, 256)
        x = jax.random.normal(k1, (B, S, D_IN), dtype=jnp.float32)
        weight = jax.random.normal(k2, (D_OUT, D_IN), dtype=jnp.float32) * 0.02
        scale_weight = jax.random.uniform(k3, (D_OUT,), dtype=jnp.float32, minval=0.5, maxval=1.5)
        bias = jax.random.normal(k4, (D_OUT,), dtype=jnp.float32) * 0.02
        return {'x': x, 'weight': weight, 'scale_weight': scale_weight, 'bias': bias}
    _L1_ffn_all = _L1_ffn_setup()
    _L1_ffn_in = {k: v for k, v in _L1_ffn_all.items() if k in ('weight', 'scale_weight', 'bias')}
    del _L1_ffn_all
    return {'x': x, 'itok_B_0_7': itok_B_0_7, 'L0_cond_weights': _L0_cond_in['weights'], 'L0_ffn_Wg': _L0_ffn_in['Wg'], 'L0_ffn_bg': _L0_ffn_in['bg'], 'L0_ffn_W1': _L0_ffn_in['W1'], 'L0_ffn_W2': _L0_ffn_in['W2'], 'L1_cond_Wg': _L1_cond_in['Wg'], 'L1_cond_Wu': _L1_cond_in['Wu'], 'L1_cond_Wd': _L1_cond_in['Wd'], 'L1_cond_Ag': _L1_cond_in['Ag'], 'L1_cond_Bg': _L1_cond_in['Bg'], 'L1_cond_Au': _L1_cond_in['Au'], 'L1_cond_Bu': _L1_cond_in['Bu'], 'L1_cond_Ad': _L1_cond_in['Ad'], 'L1_cond_Bd': _L1_cond_in['Bd'], 'L1_ffn_weight': _L1_ffn_in['weight'], 'L1_ffn_scale_weight': _L1_ffn_in['scale_weight'], 'L1_ffn_bias': _L1_ffn_in['bias']}

def reference(x, itok_B_0_7, L0_cond_weights, L0_ffn_Wg, L0_ffn_bg, L0_ffn_W1, L0_ffn_W2, L1_cond_Wg, L1_cond_Wu, L1_cond_Wd, L1_cond_Ag, L1_cond_Bg, L1_cond_Au, L1_cond_Bu, L1_cond_Ad, L1_cond_Bd, L1_ffn_weight, L1_ffn_scale_weight, L1_ffn_bias):
    import jax
    import jax.numpy as jnp

    def _L0_cond_ref(x, subjects, weights):
        import jax, jax.numpy as jnp
        import numpy as np
        B, C, D, T, N_SUBJECTS = (128, 32, 32, 256, 8)
        w = weights[subjects]
        out = jnp.einsum('bct,bcd->bdt', x, w)
        return out

    def _L0_ffn_ref(x, Wg, bg, W1, W2):
        import jax, jax.numpy as jnp
        import numpy as np
        B, T, D, E, H = (4, 256, 256, 4, 1024)
        TOPK = 2
        CAPACITY_FACTOR = 1
        Bq, Tq, Dq = x.shape
        N = Bq * Tq
        capacity = int(N * CAPACITY_FACTOR / E)
        flat_x = x.reshape(N, Dq)
        logits = flat_x @ Wg + bg
        top_vals, top_idx = jax.lax.top_k(logits, TOPK)
        sparse = jnp.full_like(logits, -jnp.inf)
        sparse = sparse.at[jnp.arange(N)[:, None], top_idx].set(top_vals)
        probs = jax.nn.softmax(sparse, axis=-1)
        out = jnp.zeros_like(flat_x)
        for i in range(E):
            assigned = (top_idx == i).any(axis=-1)
            score = jnp.where(assigned, probs[:, i], -jnp.inf)
            sel_p, sel_idx = jax.lax.top_k(score, capacity)
            p = jnp.where(jnp.isfinite(sel_p), sel_p, 0.0)[:, None]
            tok = flat_x[sel_idx]
            h = jax.nn.gelu(tok @ W1[i], approximate=False)
            y = h @ W2[i] * p
            out = out.at[sel_idx].add(y)
        return out.reshape(Bq, Tq, Dq)

    def _L1_cond_ref(x, Wg, Wu, Wd, Ag, Bg, Au, Bu, Ad, Bd, adapter_indices):
        import jax, jax.numpy as jnp
        import numpy as np

        def _lora_linear(x, W, A, B, adapter_indices):
            base = jnp.einsum('bsd,df->bsf', x, W)
            Ai = A[adapter_indices]
            Bi = B[adapter_indices]
            lora = jnp.einsum('bsr,brf->bsf', jnp.einsum('bsd,bdr->bsr', x, Ai), Bi)
            return base + lora
        gate = _lora_linear(x, Wg, Ag, Bg, adapter_indices)
        up = _lora_linear(x, Wu, Au, Bu, adapter_indices)
        h = jax.nn.silu(gate) * up
        return _lora_linear(h, Wd, Ad, Bd, adapter_indices)

    def _L1_ffn_ref(x, weight, scale_weight, bias):
        import jax, jax.numpy as jnp
        import numpy as np
        w = weight * scale_weight[:, None]
        out = jnp.einsum('bsi,oi->bso', x, w) + bias
        return out
    x = x + _L0_ffn_ref(_L0_cond_ref(x, itok_B_0_7, L0_cond_weights), L0_ffn_Wg, L0_ffn_bg, L0_ffn_W1, L0_ffn_W2)
    x = x + _L1_ffn_ref(_L1_cond_ref(x, L1_cond_Wg, L1_cond_Wu, L1_cond_Wd, L1_cond_Ag, L1_cond_Bg, L1_cond_Au, L1_cond_Bu, L1_cond_Ad, L1_cond_Bd, itok_B_0_7), L1_ffn_weight, L1_ffn_scale_weight, L1_ffn_bias)
    return x

_drawn_inputs = setup_inputs


def setup_inputs(seed=0):
    import zlib

    import numpy as np

    out = dict(_drawn_inputs(seed))
    spreads = {'L0_ffn_bg': (0.0, 0.1),
     'L1_cond_Bg': (0.009999999776482582, 0.6),
     'L1_cond_Bu': (0.009999999776482582, 0.6),
     'L1_cond_Bd': (0.009999999776482582, 0.6)}
    factors = {'L1_cond_Ag': 6.321, 'L1_cond_Au': 6.276, 'L1_cond_Ad': 6.232, 'L1_ffn_bias': 3.367}
    for name, (base, spread) in spreads.items():
        noise = np.random.default_rng([zlib.crc32(name.encode()), seed]).standard_normal(out[name].shape)
        drawn = base * np.exp(spread * noise) if base else spread * noise
        out[name] = jnp.asarray(drawn.astype(out[name].dtype))
    for name, factor in factors.items():
        out[name] = (out[name] * factor).astype(out[name].dtype)
    return out
```

```python
import concourse.bass as bass
from concourse import mybir
from contextlib import ExitStack
import numpy as np

P = 128
TOK, D, HID = 4096, 256, 1024
G = TOK // P
E, CAP = 4, 1024
Q = CAP // P
KD, KH = D // P, HID // P
BT = 512
GB = BT // P
NB0, NB1 = E * CAP // BT, TOK // BT
NAD = 8
C = 6
SB = BT // 32
MAGIC = 12582912.0
LOG2E, LN2_HI, LN2_LO = 1.4426950408889634, 0.693145751953125, 1.4286068203094173e-06
EXP_C = [1 / 5040, 1 / 720, 1 / 120, 1 / 24, 1 / 6, 0.5, 1.0]
SEARCH_STEPS = 15


def shape_constants():
    p = np.arange(P)
    restart = np.ones((P, 2 * E, G), np.float32)
    restart[:, :, 0] = 0.0
    return {
        "c_ident": np.eye(P, dtype=np.float32),
        "c_cols": np.stack([p, TOK + p, p // 16], 1).astype(np.float32),
        "c_iota": np.broadcast_to(np.arange(P, dtype=np.float32), (P, P)).copy(),
        "c_before": (p[:, None] < p[None, :]).astype(np.float32),
        "c_restart": restart.reshape(P, 2 * E * G),
        "c_steps": np.broadcast_to(np.array([1, 2, 3], np.uint32) << 28, (P, 3)).copy(),
        "c_behind": np.broadcast_to(np.repeat(np.arange(E - 1, -1, -1, dtype=np.float32), G), (P, E * G)).copy(),
    }


def adaln_moe_lora(nc, A, outT):
    f32, f32r, bf16 = mybir.dt.float32, mybir.dt.float32r, mybir.dt.bfloat16
    i32, u32 = mybir.dt.int32, mybir.dt.uint32
    ALU, ACT, AX = mybir.AluOpType, mybir.ActivationFunctionType, mybir.AxisListType

    flat_rows = nc.dram_tensor("flat_rows", (TOK + P, D), f32).ap()
    x1_rows = nc.dram_tensor("x1_rows", (TOK + P, D), f32).ap()

    ctx = ExitStack()
    with ctx:
        cursor = [(nc.sbuf_base + 63) // 64 * 64]

        def sb(name, shape, dt):
            t = nc.alloc_sbuf_tensor_at(name, shape, dt, offset=cursor[0])
            cursor[0] += (int(np.prod(shape[1:])) * (2 if dt == bf16 else 4) + 31) // 32 * 32
            assert cursor[0] <= nc.sbuf_usable_end, (name, cursor[0])
            return t

        def two(name, shape):
            return sb(name + "_hi", shape, f32r), sb(name + "_lo", shape, f32r)

        def sem(name):
            return ctx.enter_context(nc.semaphore(name))

        ident = sb("ident", [P, P], f32)
        cols = sb("cols", [P, 3], f32)
        iota = sb("iota", [P, P], f32)
        iota_b = sb("iota_b", [P, P], bf16)
        adapter_mask = sb("adapter_mask", [P, TOK // 32], f32)
        out_bias = sb("out_bias", [P, KD], f32)
        slot_row = sb("slot_row", [P, E, Q], i32)
        slot_p = sb("slot_p", [P, E, Q], f32)
        layer1_at = cursor[0]
        wg, wu = two("wg", [P, KD, HID]), two("wu", [P, KD, HID])
        wd = two("wd", [P, KH, D])
        ag, au = two("ag", [P, KD, P]), two("au", [P, KD, P])
        bg, bu = two("bg", [P, 1, HID]), two("bu", [P, 1, HID])
        ad, bd = two("ad", [P, KH, P]), two("bd", [P, 1, D])
        work_at = cursor[0]

        cursor[0] = layer1_at
        x_sb = sb("x_sb", [P, G, D + E], f32)
        mix = sb("mix", [P, G, P], f32)
        mix_row = sb("mix_row", [P, G, 32], f32)
        subj_w = sb("subj_w", [P, NAD, 32], f32)
        subj_i = sb("subj_i", [P, G], i32)
        subj_f = sb("subj_f", [P, G], f32)
        subj_is = sb("subj_is", [P, NAD, G], i32)
        xT = [sb(f"xT{i}", [P, KD, BT], f32) for i in range(2)]
        zT = sb("zT", [P, BT], f32)
        gate_w = sb("gate_w", [P, KD, 32], f32)
        flat_st = [sb(f"flat_st{i}", [P, GB, D], f32) for i in range(2)]
        assert cursor[0] <= work_at

        cursor[0] = work_at
        w1, w2 = two("w1", [P, KD, HID]), two("w2", [P, KH, D])
        w1_raw, w2_raw = sb("w1_raw", [P, KD, HID], f32), sb("w2_raw", [P, KH, D], f32)
        pos_r, pos_q = sb("pos_r", [P, E, G], bf16), sb("pos_q", [P, E, G], bf16)
        vals = sb("vals", [P, E, G, C], bf16)
        onehot_q = sb("onehot_q", [P, G, Q], bf16)
        onehot_r = sb("onehot_r", [P, G, P], bf16)
        slotted = sb("slotted", [P, G, Q, C], bf16)
        routed = sb("routed", [P, Q, C], f32)
        route_t = sb("route_t", [P, 3, Q], f32)
        late_at = cursor[0]
        xg = sb("xg", [P, GB, D], f32)
        xs = [two(f"xs{i}", [P, KD, BT]) for i in range(2)]
        hid = [two(f"hid{i}", [P, BT]) for i in range(4)]
        hf = [sb(f"hf{i}", [P, BT], f32) for i in range(2)]
        y_sb = [sb(f"y_sb{i}", [P, GB, D], f32) for i in range(2)]

        cursor[0] = late_at
        raw = {n: sb("raw_" + n, s, f32) for n, s in (
            ("wg", [P, KD, HID]), ("wu", [P, KD, HID]), ("wd", [P, KH, D]), ("ag", [P, KD, P]), ("au", [P, KD, P]),
            ("bg", [P, 1, HID]), ("bu", [P, 1, HID]), ("ad", [P, KH, P]), ("bd", [P, 1, D]))}
        wdT = sb("wdT", [P, KD, HID], f32)
        bdT = sb("bdT", [P, KD, P], f32)
        wfT = sb("wfT", [P, KD, D], f32)
        wfT_s = sb("wfT_s", [P, KD, D], f32)
        wf_scale = sb("wf_scale", [P, D], f32)
        before = sb("before", [P, P], f32)
        before_b, ones_b = sb("before_b", [P, P], bf16), sb("ones_b", [P, P], bf16)
        restart = sb("restart", [P, 2 * E * G], f32)
        steps = sb("steps", [P, 3], u32)
        gate_b = sb("gate_b", [P, E], f32)
        sample_i = sb("sample_i", [P, TOK // 32], i32)
        logit = sb("logit", [P, E, G], f32)
        rank = sb("rank", [P, E, G], f32)
        t_eg = [sb(f"t_eg{i}", [P, E, G], f32) for i in range(3)]
        t_g = [sb(f"t_g{i}", [P, G], f32) for i in range(8)]
        prob, score = sb("prob", [P, E, G], f32), sb("score", [P, E, G], f32)
        thr = sb("thr", [P, E], f32)
        cand = sb("cand", [P, E, 3], f32)
        passed = sb("passed", [P, E, 3, G], bf16)
        passed_n = sb("passed_n", [P, E, 3], bf16)
        kept = sb("kept", [P, E, 3], f32)
        best = sb("best", [P, E], f32)
        above = sb("above", [P, 2, E, G], bf16)
        incl = sb("incl", [P, 2, E, G], f32)
        prefix = sb("prefix", [P, 2, E, G], f32)
        need = sb("need", [P, E], f32)
        pos_i = [sb(f"pos_i{i}", [P, E, G], i32) for i in range(2)]

        cursor[0] = work_at
        x1_sb = [sb(f"x1_sb{i}", [P, GB, D], f32) for i in range(2)]
        x1T = [sb(f"x1T{i}", [P, KD, BT], f32) for i in range(2)]
        x1s = [two(f"x1s{i}", [P, KD, BT]) for i in range(2)]
        ug, uu = [two(f"ug{i}", [P, BT]) for i in range(2)], [two(f"uu{i}", [P, BT]) for i in range(2)]
        um = [sb(f"um{i}", [P, BT], f32) for i in range(2)]
        vm = sb("vm", [P, BT], f32)
        vs = two("vs", [P, BT])
        hid1 = [two(f"hid1_{i}", [P, BT]) for i in range(4)]
        act1 = [sb(f"act1_{i}", [P, BT], f32) for i in range(2)]
        prod = [sb(f"prod{i}", [P, BT], f32) for i in range(2)]
        out_sb = [sb(f"out_sb{i}", [P, KD, BT], f32) for i in range(2)]

        bank = [ctx.enter_context(nc.psum_tensor(f"bank{i}", [P, BT], f32)) for i in range(8)]

        x_in = [sem(f"x_in{i}") for i in range(8)]
        small_in = sem("small_in")
        raw0_in, raw1_in = sem("raw0_in"), sem("raw1_in")
        flat_out = [sem(f"flat_out{i}") for i in range(2)]
        x1_init = sem("x1_init")
        spare_out = sem("spare_out")
        zeroed = sem("zeroed")
        xT_t, xT_ev = sem("xT_t"), sem("xT_ev")
        z_mm, z_ev, z_tr, z_in = sem("z_mm"), sem("z_ev"), sem("z_tr"), sem("z_in")
        mixed = sem("mixed")
        rows_mm, rows_ev, logit_ev = sem("rows_mm"), sem("rows_ev"), sem("logit_ev")
        fold_in, fold_mm, fold_ev = sem("fold_in"), sem("fold_mm"), sem("fold_ev")
        hi0, lo0 = sem("hi0"), sem("lo0")
        hi1, lo1 = sem("hi1"), sem("lo1")
        chain = sem("chain")
        asked, counted = sem("asked"), sem("counted")
        ranks_in, ranked = sem("ranks_in"), sem("ranked")
        route_in, route_mm, route_out = sem("route_in"), sem("route_mm"), sem("route_out")
        gathered, scattered = sem("gathered"), sem("scattered")
        up0, gelu0, hi_0, hid0, down0 = sem("up0"), sem("gelu0"), sem("hi_0"), sem("hid0"), sem("down0")
        xsT, xs_hi, xs_lo = sem("xsT"), sem("xs_hi"), sem("xs_lo")
        y_out = sem("y_out")
        nw_hi, w1_new, w2_new = sem("nw_hi"), sem("w1_new"), sem("w2_new")
        x1_in = [sem(f"x1_in{i}") for i in range(2)]
        x1_t, x1_act, x1_lo = sem("x1_t"), sem("x1_act"), sem("x1_lo")
        u_mm, u_ev, u_hi, u_lo = sem("u_mm"), sem("u_ev"), sem("u_hi"), sem("u_lo")
        gate1, up1, silu1, prod1, phi1, hid1_s, down1 = (sem("gate1"), sem("up1"), sem("silu1"), sem("prod1"),
                                                         sem("phi1"), sem("hid1"), sem("down1"))
        v_ev, v_hi, v_lo = sem("v_ev"), sem("v_hi"), sem("v_lo")
        acc1, out_ev = sem("acc1"), sem("out_ev")
        out_done = [sem(f"out_done{i}") for i in range(2)]

        SPLITS = [(raw[n], w) for n, w in (("wg", wg), ("wu", wu), ("ag", ag), ("au", au), ("bg", bg), ("bu", bu),
                                           ("ad", ad), ("wd", wd), ("bd", bd))]
        NPLAIN = 7

        def pieces(t):
            n = max(1, 1024 // t.shape[2])
            return [slice(a, min(a + n, t.shape[1])) for a in range(0, t.shape[1], n)]

        NP1 = sum(len(pieces(r)) for r, _ in SPLITS)
        NP_PLAIN = sum(len(pieces(r)) for r, _ in SPLITS[:NPLAIN])
        SMALL = 0

        block = ctx.enter_context(nc.Block())

        @block.sync
        def _(sp):
            nonlocal SMALL

            def small(dst, src):
                nonlocal SMALL
                sp.dma_start(dst, src).then_inc(small_in, 16)
                SMALL += 16

            small(ident[:, :], A["c_ident"])
            for k in range(KD):
                small(gate_w[:, k, 0:E], A["L0_ffn_Wg"][k * P:(k + 1) * P, :])
            for s in range(4):
                small(subj_w[32 * s:32 * s + 32, :, :], A["L0_cond_weights"].rearrange("a c d -> c a d"))
                small(subj_i[32 * s:32 * s + 32, :], A["itok_by_place"][s:s + 1, :].partition_broadcast(32))
            def load_x(i):
                src = x_view[i * GB:(i + 1) * GB].rearrange("g p d -> p g d")
                sp.dma_start(x_sb[:, i * GB:(i + 1) * GB, 0:D], src).then_inc(x_in[i], 16)
            x_view = A["x"].rearrange("(g p) d -> g p d", p=P)
            for i in range(3):
                load_x(i)
            small(cols[:, :], A["c_cols"])
            small(iota[:, :], A["c_iota"])
            small(before[:, :], A["c_before"])
            small(restart[:, :], A["c_restart"])
            small(steps[:, :], A["c_steps"])
            small(rank[:, :, :], A["c_behind"].rearrange("p (e g) -> p e g", e=E))
            small(sample_i[:, :], A["itok"].partition_broadcast(P))
            small(gate_b[:, :], A["L0_ffn_bg"].partition_broadcast(P))
            small(wf_scale[:, :], A["L1_ffn_scale_weight"].partition_broadcast(P))
            small(out_bias[:, :], A["out_bias_cols"])
            for i in range(3, 8):
                load_x(i)

            def load_expert(e, done):
                sp.dma_start(w1_raw[:, :, :], A["L0_ffn_W1"][e].rearrange("(k p) n -> p k n", p=P)).then_inc(done, 16)
                sp.dma_start(w2_raw[:, :, :], A["L0_ffn_W2"][e].rearrange("(k p) n -> p k n", p=P)).then_inc(done, 16)

            load_expert(0, raw0_in)
            for dst, src in ((wfT, A["wfT"]), (wdT, A["wdT"]), (bdT, A["bdT"])):
                sp.dma_start(dst[:, :, :], src.rearrange("(k p) n -> p k n", p=P)).then_inc(raw1_in, 16)
            for n, src in (("wg", A["L1_cond_Wg"]), ("wu", A["L1_cond_Wu"]), ("ag", A["ag_all"]), ("au", A["au_all"]),
                           ("bg", A["bg_all"]), ("bu", A["bu_all"]), ("ad", A["ad_all"])):
                sp.dma_start(raw[n][:, :, :], src.rearrange("(k p) n -> p k n", p=P)).then_inc(raw1_in, 16)

            x1_v = x1_rows[0:TOK].rearrange("(g p) d -> p g d", p=P)
            flat_v = flat_rows[0:TOK].rearrange("(g p) d -> p g d", p=P)
            for i in range(8):
                sp.wait_ge(x_in[i], 16)
                sp.dma_start(x1_v[:, i * GB:(i + 1) * GB, :], x_sb[:, i * GB:(i + 1) * GB, 0:D]).then_inc(x1_init, 16)
            sp.wait_ge(zeroed, 3)
            sp.dma_start(x1_rows[TOK:TOK + P, :], zT[:, 0:D]).then_inc(spare_out, 16)
            sp.dma_start(flat_rows[TOK:TOK + P, :], zT[:, 0:D]).then_inc(spare_out, 16)
            for i in range(8):
                sp.wait_ge(rows_ev, (i + 1) * GB)
                sp.dma_start(flat_v[:, i * GB:(i + 1) * GB, :], flat_st[i % 2][:, :, :]).then_inc(flat_out[i % 2], 16)
            for e in range(1, E):
                if e == 1:
                    sp.wait_ge(lo0, 4)
                else:
                    sp.wait_ge(w1_new, KH * (e - 1))
                    sp.wait_ge(w2_new, KH * (e - 1))
                load_expert(e, raw0_in)
            x1_b = x1_rows[0:TOK].rearrange("(t g p) d -> t p g d", p=P, g=GB)
            out_v = outT.rearrange("k p (t n) -> t p k n", n=BT)
            sp.wait_ge(scattered, 16 * GB * NB0)
            for t in range(2):
                sp.dma_start(x1_sb[t][:, :, :], x1_b[t]).then_inc(x1_in[t], 16)
            for t in range(NB1):
                if t + 2 < NB1:
                    sp.wait_ge(x1_t, KD * (t + 1))
                    sp.dma_start(x1_sb[t % 2][:, :, :], x1_b[t + 2]).then_inc(x1_in[t % 2], 16)
                sp.wait_ge(out_ev, KD * (t + 1))
                sp.dma_start(out_v[t], out_sb[t % 2][:, :, :]).then_inc(out_done[t % 2], 16)
            for i in range(2):
                sp.wait_ge(out_done[i], 16 * NB1 // 2)

        @block.gpsimd
        def _(pool):
            pool.memset(gate_w[:, :, E:32], 0.0).then_inc(zeroed, 1)
            pool.memset(mix[:, :, :], 0.0).then_inc(zeroed, 1)
            pool.memset(zT[:, 0:D], 0.0).then_inc(zeroed, 1)
            pool.wait_ge(raw0_in, 32)
            n = 0
            for r, (hi, lo) in ((w1_raw, w1), (w2_raw, w2)):
                for a in pieces(r):
                    n += 1
                    pool.wait_ge(hi0, n)
                    pool.tensor_tensor(lo[:, a, :], r[:, a, :], hi[:, a, :].bitcast(f32), ALU.subtract).then_inc(lo0, 1)
            n = 0
            for r, (hi, lo) in SPLITS:
                for a in pieces(r):
                    n += 1
                    pool.wait_ge(hi1, n)
                    pool.tensor_tensor(lo[:, a, :], r[:, a, :], hi[:, a, :].bitcast(f32), ALU.subtract).then_inc(lo1, 1)

            def gather(b):
                e, half = b // 2, b % 2
                pool.wait_ge(route_out, e + 1)
                if b:
                    pool.wait_ge(xsT, KD * b)
                for q in range(GB):
                    pool.indirect_dma_start(
                        out=xg[:, q, :], out_offset=None, in_=flat_rows[:, :],
                        in_offset=bass.IndirectOffsetOnAxis(ap=slot_row[:, e, half * GB + q:half * GB + q + 1], axis=0),
                    ).then_inc(gathered, 16)

            def scatter(b):
                e, half = b // 2, b % 2
                pool.wait_ge(y_out, b + 1)
                for q in range(GB):
                    if b or q:
                        pool.wait_ge(scattered, 16 * (GB * b + q))
                    pool.indirect_dma_start(
                        out=x1_rows[:, :],
                        out_offset=bass.IndirectOffsetOnAxis(ap=slot_row[:, e, half * GB + q:half * GB + q + 1], axis=0),
                        in_=y_sb[half][:, q, :], in_offset=None, compute_op=ALU.add).then_inc(scattered, 16)

            for i in range(2):
                pool.wait_ge(flat_out[i], 64)
            pool.wait_ge(spare_out, 32)
            pool.wait_ge(x1_init, 128)
            pool.wait_ge(lo1, NP1)
            gather(0)
            for b in range(NB0):
                if b + 1 < NB0:
                    gather(b + 1)
                if b:
                    scatter(b - 1)
            scatter(NB0 - 1)

        @block.scalar
        def _(act):
            act.wait_ge(small_in, SMALL)
            for i in range(8):
                for k in range(KD):
                    act.wait_ge(xT_t, KD * i + k + 1)
                    if i >= 2 and k == 0:
                        act.wait_ge(z_mm, i - 1)
                    act.activation(xT[i % 2][:, k, :], bank[k][:, :], ACT.Copy).then_inc(xT_ev, 1)
                if i % 4 == 3:
                    act.wait_ge(z_mm, i + 1)
                    if i == 3:
                        act.wait_ge(spare_out, 32)
                    else:
                        act.wait_ge(z_tr, 1)
                    act.activation(zT[:, :], bank[2][:, :], ACT.Copy).then_inc(z_ev, 1)
            for g in range(G):
                act.wait_ge(rows_mm, g + 1)
                if g >= 2 * GB and g % GB == 0:
                    act.wait_ge(flat_out[g // GB % 2], 16 * (g // GB // 2))
                act.activation(flat_st[g // GB % 2][:, g % GB, :], bank[4 + g % 4][:, 0:D], ACT.Copy).then_inc(rows_ev, 1)
            act.wait_ge(raw0_in, 32)
            for r, (hi, lo) in ((w1_raw, w1), (w2_raw, w2)):
                for a in pieces(r):
                    act.activation(hi[:, a, :], r[:, a, :], ACT.Copy).then_inc(hi0, 1)
            act.wait_ge(raw1_in, 160)
            act.wait_ge(logit_ev, G)
            act.wait_ge(x1_init, 128)
            for i in range(2):
                act.wait_ge(flat_out[i], 64)
            for r, (hi, lo) in SPLITS[:NPLAIN]:
                for a in pieces(r):
                    act.activation(hi[:, a, :], r[:, a, :], ACT.Copy).then_inc(hi1, 1)
            for j in range(KH // 2):
                act.wait_ge(fold_mm, j + 1)
                act.activation(raw["wd"][:, 2 * j:2 * j + 2, :], bank[j][:, :].rearrange("p (a n) -> p a n", a=2),
                               ACT.Copy).then_inc(fold_ev, 1)
            act.wait_ge(fold_mm, KH // 2 + 1)
            act.activation(raw["bd"][:, 0, :], bank[5][:, 0:D], ACT.Copy).then_inc(fold_ev, 1)
            act.wait_ge(fold_ev, KH // 2 + 1)
            for r, (hi, lo) in SPLITS[NPLAIN:]:
                for a in pieces(r):
                    act.activation(hi[:, a, :], r[:, a, :], ACT.Copy).then_inc(hi1, 1)

            def slots_hi(b, k):
                act.wait_ge(xsT, KD * b + k + 1)
                act.activation(xs[b % 2][0][:, k, :], bank[6][:, :], ACT.Copy).then_inc(xs_hi, 1)

            def rows_of_y(b):
                e = b // 2
                act.wait_ge(down0, KH * (b + 1))
                if b >= 2:
                    act.wait_ge(scattered, 16 * GB * (b - 1))
                for q in range(GB):
                    src = bank[2 + 2 * (b % 2) + q // 2][:, (q % 2) * D:(q % 2 + 1) * D]
                    last = act.activation(y_sb[b % 2][:, q, :], src, ACT.Copy,
                                          scale=slot_p[:, e, (b % 2) * GB + q:(b % 2) * GB + q + 1])
                last.then_inc(y_out, 1)

            act.wait_ge(lo1, NP1)
            for k in range(KD):
                slots_hi(0, k)
            for b in range(NB0):
                for h in range(KH):
                    s = KH * b + h
                    act.wait_ge(up0, s + 1)
                    if s >= 2:
                        act.wait_ge(hid0, s - 1)
                    act.activation(hf[s % 2][:, :], bank[s % 2][:, :], ACT.Gelu).then_inc(gelu0, 1)
                    if h == 1 and b:
                        rows_of_y(b - 1)
                    if h in (5, 7) and b + 1 < NB0:
                        slots_hi(b + 1, h // 2 - 2)
                    if b % 2 and b < NB0 - 1:
                        if h == 0:
                            act.wait_ge(raw0_in, 32 * (b // 2 + 2))
                        hc = slice(h * P, (h + 1) * P)
                        act.activation(w1[0][:, :, hc], w1_raw[:, :, hc], ACT.Copy).then_inc(nw_hi, 1)
                        if h >= 2:
                            act.wait_ge(down0, s - 1)
                            act.activation(w2[0][:, h - 2, :], w2_raw[:, h - 2, :], ACT.Copy).then_inc(nw_hi, 1)
                    if b and b % 2 == 0 and h < 2:
                        act.wait_ge(down0, s - 1)
                        act.activation(w2[0][:, KH - 2 + h, :], w2_raw[:, KH - 2 + h, :], ACT.Copy).then_inc(nw_hi, 1)
            rows_of_y(NB0 - 1)

            def x1_parts(par, n, k):
                act.wait_ge(x1_t, n)
                act.activation(x1T[par][:, k, :], bank[7][:, :], ACT.Copy)
                act.activation(x1s[par][0][:, k, :], bank[7][:, :], ACT.Copy).then_inc(x1_act, 1)

            def steps1(t, par, first, last):
                for h in range(KH):
                    s = KH * t + h
                    act.wait_ge(gate1, s + 1)
                    if not (first and h < 2):
                        act.wait_ge(prod1, s - 1)
                    act.activation(act1[h % 2][:, :], bank[h % 2][:, :], ACT.Silu).then_inc(silu1, 1)
                    if h in (3, 4) and not last:
                        if h == 3 and not first:
                            act.wait_ge(out_ev, KD * t)
                        x1_parts(1 - par, KD * (t + 1) + h - 2, h - 3)

            for k in range(KD):
                x1_parts(0, k + 1, k)
            steps1(0, 0, True, False)
            steps1(1, 1, False, False)
            with act.Fori(1, NB1 // 2 - 1) as i:
                steps1(2 * i, 0, False, False)
                steps1(2 * i + 1, 1, False, False)
            steps1(NB1 - 2, 0, False, False)
            steps1(NB1 - 1, 1, False, True)

        @block.vector
        def _(dve):
            n_chain = 0

            def link(ins):
                nonlocal n_chain
                n_chain += 1
                ins.then_inc(chain, 1)
                dve.wait_ge(chain, n_chain)

            def over(ap, n):
                return ap.unsqueeze(len(ap.shape)).to_broadcast(list(ap.shape) + [n])

            dve.wait_ge(small_in, SMALL)
            link(dve.tensor_copy(subj_f[:, :], subj_i[:, :]))
            link(dve.tensor_tensor(subj_is[:, :, :], subj_f[:, :].unsqueeze(1).to_broadcast([P, NAD, G]),
                                   over(iota[:, 0:NAD], G), ALU.is_equal))
            link(dve.memset(mix_row[:, :, :], 0.0))
            for a in range(NAD):
                link(dve.copy_predicated(mix_row[:, :, :], over(subj_is[:, a, :], 32),
                                         subj_w[:, a, :].unsqueeze(1).to_broadcast([P, G, 32])))
            dve.wait_ge(zeroed, 3)
            for s in range(4):
                r = slice(32 * s, 32 * s + 32)
                dve.tensor_copy(mix[r, :, r], mix_row[r, :, :]).then_inc(mixed, 1)
            dve.tensor_copy(iota_b[:, :], iota[:, :])
            dve.tensor_copy(before_b[:, :], before[:, :])
            dve.memset(ones_b[:, :], 1.0)
            link(dve.memset(thr[:, :], 0.0))
            for s in range(2):
                dve.wait_ge(z_tr, s + 1)
                dst = x_sb[:, s * 16:(s + 1) * 16, D:D + E].rearrange("p (j c) e -> p j c e", j=4)
                src = bank[3][:, :].rearrange("p (c j r) -> p j c r", c=4, j=4)[:, :, :, 0:E]
                dve.tensor_copy(dst, src).then_inc(z_in, 1)
            dve.wait_ge(raw1_in, 160)
            dve.tensor_tensor(wfT_s[:, :, :], wfT[:, :, :], wf_scale[:, :].unsqueeze(1).to_broadcast([P, KD, D]),
                              ALU.mult).then_inc(fold_in, 1)
            link(dve.tensor_copy(adapter_mask[:, :], sample_i[:, :]))
            link(dve.tensor_scalar(adapter_mask[:, :], adapter_mask[:, :], cols[:, 2:3], None, ALU.is_equal))
            for g in range(G):
                dve.wait_ge(rows_ev, g + 1)
                dve.tensor_tensor(logit[:, :, g], bank[4 + g % 4][:, D:D + E], gate_b[:, :], ALU.add).then_inc(logit_ev, 1)
            dve.wait_ge(logit_ev, G)
            for d in range(1, E):
                link(dve.tensor_tensor(t_eg[0][:, 0:E - d, :], logit[:, 0:E - d, :], logit[:, d:E, :], ALU.is_ge))
                link(dve.tensor_tensor(rank[:, d:E, :], rank[:, d:E, :], t_eg[0][:, 0:E - d, :], ALU.add))
                link(dve.tensor_tensor(rank[:, 0:E - d, :], rank[:, 0:E - d, :], t_eg[0][:, 0:E - d, :], ALU.subtract))
            m1, m2, neg, n_f, r_, t_, p1, p2 = t_g
            dve.tensor_reduce(m1[:, :], logit[:, :, :].rearrange("p e g -> p g e"), AX.X, ALU.max)
            link(dve.scalar_tensor_tensor(t_eg[0][:, :, :], rank[:, :, :], 1.0, logit[:, :, :], ALU.is_equal, ALU.mult))
            link(dve.tensor_reduce(m2[:, :], t_eg[0][:, :, :].rearrange("p e g -> p g e"), AX.X, ALU.add))
            link(dve.tensor_tensor(neg[:, :], m2[:, :], m1[:, :], ALU.subtract))
            link(dve.tensor_scalar(neg[:, :], neg[:, :], -87.0, None, ALU.max))
            link(dve.tensor_scalar(n_f[:, :], neg[:, :], LOG2E, MAGIC + 127.0, ALU.mult, ALU.add))
            link(dve.tensor_scalar(p1[:, :], n_f[:, :], -(MAGIC + 127.0), None, ALU.add))
            link(dve.scalar_tensor_tensor(r_[:, :], p1[:, :], -LN2_HI, neg[:, :], ALU.mult, ALU.add))
            link(dve.scalar_tensor_tensor(r_[:, :], p1[:, :], -LN2_LO, r_[:, :], ALU.mult, ALU.add))
            link(dve.tensor_scalar(t_[:, :], r_[:, :], EXP_C[0], None, ALU.mult))
            for c in EXP_C[1:]:
                link(dve.scalar_tensor_tensor(t_[:, :], t_[:, :], c, r_[:, :], ALU.add, ALU.mult))
            link(dve.tensor_scalar(t_[:, :], t_[:, :], 1.0, None, ALU.add))
            link(dve.tensor_scalar(n_f[:, :].bitcast(u32), n_f[:, :].bitcast(u32), 23, None, ALU.logical_shift_left))
            link(dve.tensor_tensor(t_[:, :], t_[:, :], n_f[:, :], ALU.mult))
            link(dve.tensor_scalar(m1[:, :], t_[:, :], 1.0, None, ALU.add))
            link(dve.reciprocal(p1[:, :], m1[:, :]))
            link(dve.tensor_tensor(p2[:, :], t_[:, :], p1[:, :], ALU.mult))
            for i, p_ in ((0, p1), (1, p2)):
                link(dve.scalar_tensor_tensor(t_eg[i][:, :, :], rank[:, :, :], float(i),
                                              p_[:, :].unsqueeze(1).to_broadcast([P, E, G]), ALU.is_equal, ALU.mult))
            link(dve.tensor_tensor(prob[:, :, :], t_eg[0][:, :, :], t_eg[1][:, :, :], ALU.add))
            link(dve.tensor_scalar(t_eg[2][:, :, :], rank[:, :, :], 2.0, None, ALU.is_ge))
            link(dve.tensor_tensor(score[:, :, :], prob[:, :, :], t_eg[2][:, :, :], ALU.subtract))

            base = n_chain
            OWN = 6
            with dve.Fori(0, SEARCH_STEPS) as it:
                def own(ins, k):
                    ins.then_inc(chain, 1)
                    dve.wait_ge(chain, it * OWN + (base + k))
                own(dve.tensor_tensor(cand[:, :, :].bitcast(u32), over(thr[:, :].bitcast(u32), 3),
                                      steps[:, :].unsqueeze(1).to_broadcast([P, E, 3]), ALU.bitwise_or), 1)
                own(dve.tensor_tensor(passed[:, :, :, :], score[:, :, :].unsqueeze(2).to_broadcast([P, E, 3, G]),
                                      over(cand[:, :, :], G), ALU.is_ge), 2)
                with nc.allow_low_precision("counts up to 32"):
                    dve.tensor_reduce(passed_n[:, :, :], passed[:, :, :, :], AX.X, ALU.add).then_inc(asked, 1)
                own(dve.tensor_scalar(steps[:, :], steps[:, :], 2, None, ALU.logical_shift_right), 3)
                dve.wait_ge(counted, it + 1)
                own(dve.scalar_tensor_tensor(kept[:, :, :], bank[4][:, 0:3 * E].rearrange("p (e j) -> p e j", j=3),
                                             float(CAP), cand[:, :, :], ALU.is_ge, ALU.mult), 4)
                own(dve.tensor_reduce(best[:, :], kept[:, :, :], AX.X, ALU.max), 5)
                own(dve.tensor_tensor(thr[:, :], thr[:, :], best[:, :], ALU.max), 6)
            n_chain = base + SEARCH_STEPS * OWN

            thr_b = over(thr[:, :], G)
            dve.tensor_tensor(above[:, 0, :, :], score[:, :, :], thr_b, ALU.is_gt)
            dve.tensor_tensor(above[:, 1, :, :], score[:, :, :], thr_b, ALU.is_equal).then_inc(ranks_in, 1)
            dve.wait_ge(ranked, 2)
            flat2 = lambda t: t[:, :, :, :].rearrange("p a e g -> p (a e g)")
            link(dve.tensor_tensor_scan(flat2(incl), restart[:, :], bank[6][:, 0:2 * E * G], 0.0, ALU.mult, ALU.add))
            link(dve.tensor_tensor(flat2(prefix), flat2(incl), bank[6][:, 0:2 * E * G], ALU.subtract))
            link(dve.tensor_tensor(flat2(prefix), flat2(prefix), bank[5][:, 0:2 * E * G], ALU.add))
            link(dve.tensor_scalar(need[:, :], incl[:, 0, :, G - 1], -1.0, float(CAP), ALU.mult, ALU.add))
            need_b = over(need[:, :], G)
            link(dve.tensor_tensor(t_eg[0][:, :, :], prefix[:, 1, :, :], need_b, ALU.is_lt))
            link(dve.tensor_tensor(t_eg[0][:, :, :], t_eg[0][:, :, :], above[:, 1, :, :], ALU.mult))
            link(dve.tensor_tensor(t_eg[0][:, :, :], t_eg[0][:, :, :], above[:, 0, :, :], ALU.add))
            link(dve.tensor_tensor(t_eg[1][:, :, :], prefix[:, 1, :, :], need_b, ALU.min))
            link(dve.tensor_tensor(pos_i[0][:, :, :], t_eg[1][:, :, :], prefix[:, 0, :, :], ALU.add))
            link(dve.tensor_scalar(pos_i[1][:, :, :], pos_i[0][:, :, :], 7, None, ALU.logical_shift_right))
            link(dve.tensor_scalar(pos_i[0][:, :, :], pos_i[0][:, :, :], 127, None, ALU.bitwise_and))
            dve.tensor_copy(pos_r[:, :, :], pos_i[0][:, :, :])
            link(dve.tensor_scalar(t_eg[0][:, :, :], t_eg[0][:, :, :], -64.0, 64.0, ALU.mult, ALU.add))
            link(dve.tensor_tensor(pos_q[:, :, :], pos_i[1][:, :, :], t_eg[0][:, :, :], ALU.add))
            dve.tensor_copy(vals[:, :, :, 0], over(cols[:, 0:1], G).to_broadcast([P, E, G]))
            dve.tensor_copy(vals[:, :, :, 1], iota[:, 0:G].unsqueeze(1).to_broadcast([P, E, G]))
            dve.memset(vals[:, :, :, 2], 1.0)
            link(dve.tensor_copy(vals[:, :, :, 3], prob[:, :, :]))
            link(dve.tensor_tensor(t_eg[1][:, :, :], prob[:, :, :], vals[:, :, :, 3], ALU.subtract))
            link(dve.tensor_copy(vals[:, :, :, 4], t_eg[1][:, :, :]))
            link(dve.tensor_tensor(vals[:, :, :, 5], t_eg[1][:, :, :], vals[:, :, :, 4], ALU.subtract))

            def route_make(e, part, parts=1):
                g = slice(part * G // parts, (part + 1) * G // parts)
                n = G // parts
                link(dve.tensor_tensor(onehot_q[:, g, :], over(pos_q[:, e, g], Q),
                                       iota_b[:, 0:Q].unsqueeze(1).to_broadcast([P, n, Q]), ALU.is_equal))
                dve.tensor_tensor(slotted[:, g, :, :], over(onehot_q[:, g, :], C),
                                  vals[:, e, g, :].unsqueeze(2).to_broadcast([P, n, Q, C]), ALU.mult)
                dve.tensor_tensor(onehot_r[:, g, :], over(pos_r[:, e, g], P),
                                  iota_b[:, :].unsqueeze(1).to_broadcast([P, n, P]), ALU.is_equal).then_inc(route_in, 1)

            def route_read(e):
                dve.wait_ge(route_mm, e + 1)
                link(dve.tensor_copy(routed[:, :, :], bank[7][:, 0:Q * C].rearrange("p (q c) -> p q c", c=C)))
                link(dve.scalar_tensor_tensor(route_t[:, 0, :], routed[:, :, 1], float(P), routed[:, :, 0], ALU.mult, ALU.add))
                link(dve.tensor_scalar(route_t[:, 1, :], routed[:, :, 2], -1.0, 1.0, ALU.mult, ALU.add))
                link(dve.scalar_tensor_tensor(slot_row[:, e, :], route_t[:, 1, :], cols[:, 1:2], route_t[:, 0, :], ALU.mult, ALU.add))
                link(dve.tensor_tensor(route_t[:, 2, :], routed[:, :, 3], routed[:, :, 4], ALU.add))
                dve.tensor_tensor(slot_p[:, e, :], route_t[:, 2, :], routed[:, :, 5], ALU.add).then_inc(route_out, 1)

            route_make(0, 0)
            route_read(0)

            def slots_lo(b, k):
                dve.wait_ge(xs_hi, KD * b + k + 1)
                hi, lo = xs[b % 2]
                dve.tensor_tensor(lo[:, k, :], bank[6][:, :], hi[:, k, :].bitcast(f32), ALU.subtract).then_inc(xs_lo, 1)

            n_new = 0

            def new_lo(lo, hi, r, done):
                nonlocal n_new
                n_new += 1
                dve.wait_ge(nw_hi, n_new)
                dve.tensor_tensor(lo, r, hi.bitcast(f32), ALU.subtract).then_inc(done, 1)

            for k in range(KD):
                slots_lo(0, k)
            for b in range(NB0):
                for h in range(KH):
                    s = KH * b + h
                    hi, lo = hid[s % 4]
                    dve.wait_ge(gelu0, s + 1)
                    if s >= 4:
                        dve.wait_ge(down0, s - 3)
                    dve.tensor_copy(hi[:, :], hf[s % 2][:, :]).then_inc(hi_0, 1)
                    dve.wait_ge(hi_0, s + 1)
                    dve.tensor_tensor(lo[:, :], hf[s % 2][:, :], hi[:, :].bitcast(f32), ALU.subtract).then_inc(hid0, 1)
                    if h in (5, 7) and b + 1 < NB0:
                        slots_lo(b + 1, h // 2 - 2)
                    if b < E - 1 and 1 <= h < 5:
                        if h == 1 and b:
                            dve.wait_ge(route_mm, b + 1)
                        route_make(b + 1, h - 1, 4)
                    if b < E - 1 and h == 7:
                        route_read(b + 1)
                    if b % 2 and b < NB0 - 1:
                        hc = slice(h * P, (h + 1) * P)
                        new_lo(w1[1][:, :, hc], w1[0][:, :, hc], w1_raw[:, :, hc], w1_new)
                        if h >= 2:
                            new_lo(w2[1][:, h - 2, :], w2[0][:, h - 2, :], w2_raw[:, h - 2, :], w2_new)
                    if b and b % 2 == 0 and h < 2:
                        new_lo(w2[1][:, KH - 2 + h, :], w2[0][:, KH - 2 + h, :], w2_raw[:, KH - 2 + h, :], w2_new)

            def masked(dst, src, t):
                m = adapter_mask[:, bass.ds(t * SB, SB)]
                return dve.tensor_tensor(dst[:, :].rearrange("p (s n) -> p s n", n=32),
                                         src[:, :].rearrange("p (s n) -> p s n", n=32), over(m, 32), ALU.mult)

            def x1_low(par, n, k):
                dve.wait_ge(x1_act, n)
                dve.tensor_tensor(x1s[par][1][:, k, :], x1T[par][:, k, :], x1s[par][0][:, k, :].bitcast(f32),
                                  ALU.subtract).then_inc(x1_lo, 1)

            def u_parts(t, par, j, parts):
                n = 2 * t + j + 1
                dve.wait_ge(u_mm, n)
                masked(um[j], bank[7], t).then_inc(u_ev, 1)
                dve.wait_ge(u_ev, n)
                dve.tensor_copy(parts[0][:, :], um[j][:, :]).then_inc(u_hi, 1)
                dve.wait_ge(u_hi, n)
                dve.tensor_tensor(parts[1][:, :], um[j][:, :], parts[0][:, :].bitcast(f32), ALU.subtract).then_inc(u_lo, 1)

            def finish_v(t):
                dve.wait_ge(down1, KH * (t + 1))
                masked(vm, bank[6], t).then_inc(v_ev, 1)
                dve.wait_ge(v_ev, t + 1)
                dve.tensor_copy(vs[0][:, :], vm[:, :]).then_inc(v_hi, 1)
                dve.wait_ge(v_hi, t + 1)
                dve.tensor_tensor(vs[1][:, :], vm[:, :], vs[0][:, :].bitcast(f32), ALU.subtract).then_inc(v_lo, 1)

            def finish_out(t, par, wait_store):
                dve.wait_ge(acc1, t + 1)
                if wait_store is not None:
                    dve.wait_ge(out_done[par], wait_store)
                for k in range(KD):
                    dve.scalar_tensor_tensor(out_sb[par][:, k, :], bank[4 + k][:, :], out_bias[:, k:k + 1],
                                             x1T[par][:, k, :], ALU.add, ALU.add).then_inc(out_ev, 1)

            def steps1(t, par, pair, first, last):
                for h in range(KH):
                    s = KH * t + h
                    if h == 2 and not first:
                        before_ = pair if par else pair - 1
                        prior = None if isinstance(pair, int) and before_ <= 0 else 16 * before_
                        finish_out(t - 1, 1 - par, prior)
                    dve.wait_ge(up1, s + 1)
                    dve.wait_ge(silu1, s + 1)
                    if not (first and h < 2):
                        dve.wait_ge(hid1_s, s - 1)
                    dve.tensor_tensor(prod[h % 2][:, :], bank[2 + h % 2][:, :], act1[h % 2][:, :], ALU.mult).then_inc(prod1, 1)
                    dve.wait_ge(prod1, s + 1)
                    if not (first and h < 4):
                        dve.wait_ge(down1, s - 3)
                    dve.tensor_copy(hid1[h % 4][0][:, :], prod[h % 2][:, :]).then_inc(phi1, 1)
                    dve.wait_ge(phi1, s + 1)
                    dve.tensor_tensor(hid1[h % 4][1][:, :], prod[h % 2][:, :], hid1[h % 4][0][:, :].bitcast(f32),
                                      ALU.subtract).then_inc(hid1_s, 1)
                    if h == 1 and not first:
                        finish_v(t - 1)
                    if h in (3, 4) and not last:
                        x1_low(1 - par, KD * (t + 1) + h - 2, h - 3)
                    if h == 5 and not last:
                        u_parts(t + 1, 1 - par, 0, ug[1 - par])
                    if h == 6 and not last:
                        u_parts(t + 1, 1 - par, 1, uu[1 - par])

            for k in range(KD):
                x1_low(0, k + 1, k)
            u_parts(0, 0, 0, ug[0])
            u_parts(0, 0, 1, uu[0])
            steps1(0, 0, 0, True, False)
            steps1(1, 1, 0, False, False)
            with dve.Fori(1, NB1 // 2 - 1) as i:
                steps1(2 * i, 0, i, False, False)
                steps1(2 * i + 1, 1, i, False, False)
            steps1(NB1 - 2, 0, NB1 // 2 - 1, False, False)
            steps1(NB1 - 1, 1, NB1 // 2 - 1, False, True)
            finish_v(NB1 - 1)
            finish_out(NB1 - 1, 1, 16 * (NB1 // 2 - 1))

        @block.tensor
        def _(pe):
            def product(out, lhs, rhs, start, stop):
                (lh, ll), (rh, rl) = lhs, rhs
                pe.matmul(out, lh, rh, start=start, stop=False, skip_group_check=True)
                pe.matmul(out, lh, rl, start=False, stop=False, skip_group_check=True)
                return pe.matmul(out, ll, rh, start=False, stop=stop, skip_group_check=True)

            def at(parts, *index):
                return tuple(p[index] for p in parts)

            every = slice(None)
            pe.wait_ge(small_in, SMALL)
            pe.wait_ge(zeroed, 3)
            for i in range(8):
                pe.wait_ge(x_in[i], 16)
                for k in range(KD):
                    if i:
                        pe.wait_ge(xT_ev, KD * (i - 1) + k + 1)
                    for c in range(GB):
                        last = pe.transpose(bank[k][:, c * P:(c + 1) * P], x_sb[:, i * GB + c, k * P:(k + 1) * P], ident[:, :])
                    last.then_inc(xT_t, 1)
                if i == 4:
                    pe.wait_ge(z_ev, 1)
                pe.wait_ge(xT_ev, KD * (i + 1))
                j = i % 4
                for k in range(KD):
                    last = pe.matmul(bank[2][32 * j:32 * j + 32, :], gate_w[:, k, :], xT[i % 2][:, k, :],
                                     start=k == 0, stop=k == KD - 1, tile_position=(0, 32 * j))
                last.then_inc(z_mm, 1)
                if i % 4 == 3:
                    pe.wait_ge(z_ev, i // 4 + 1)
                    if i == 7:
                        pe.wait_ge(z_in, 1)
                    for c in range(GB):
                        last = pe.transpose(bank[3][:, c * P:(c + 1) * P], zT[:, c * P:(c + 1) * P], ident[:, :])
                    last.then_inc(z_tr, 1)
            pe.wait_ge(mixed, 4)
            for g in range(G):
                if g % 16 == 0:
                    pe.wait_ge(z_in, g // 16 + 1)
                if g >= 4:
                    pe.wait_ge(rows_ev, g - 3)
                    pe.wait_ge(logit_ev, g - 3)
                pe.matmul(bank[4 + g % 4][:, 0:D + E], mix[:, g, :], x_sb[:, g, :], start=True, stop=True).then_inc(rows_mm, 1)
            pe.wait_ge(fold_in, 1)
            for h in range(KH):
                for k in range(KD):
                    last = pe.matmul(bank[h // 2][:, (h % 2) * D:(h % 2 + 1) * D], wdT[:, k, h * P:(h + 1) * P],
                                     wfT_s[:, k, :], start=k == 0, stop=k == KD - 1)
                if h % 2:
                    last.then_inc(fold_mm, 1)
            pe.wait_ge(rows_ev, G)
            pe.wait_ge(logit_ev, G)
            for k in range(KD):
                last = pe.matmul(bank[5][:, 0:D], bdT[:, k, :], wfT_s[:, k, :], start=k == 0, stop=k == KD - 1)
            last.then_inc(fold_mm, 1)
            with pe.Fori(0, SEARCH_STEPS) as it:
                pe.wait_ge(asked, it + 1)
                pe.matmul(bank[4][:, 0:3 * E], ones_b[:, :], passed_n[:, :, :].rearrange("p e j -> p (e j)"),
                          start=True, stop=True).then_inc(counted, 1)
            pe.wait_ge(fold_ev, KH // 2 + 1)
            pe.wait_ge(ranks_in, 1)
            marks = above[:, :, :, :].rearrange("p a e g -> p (a e g)")
            pe.matmul(bank[5][:, 0:2 * E * G], before_b[:, :], marks, start=True, stop=True).then_inc(ranked, 1)
            pe.matmul(bank[6][:, 0:2 * E * G], ones_b[:, :], marks, start=True, stop=True).then_inc(ranked, 1)

            def route(e, n):
                pe.wait_ge(route_in, n)
                if e:
                    pe.wait_ge(route_out, e)
                for g in range(G):
                    last = pe.matmul(bank[7][:, 0:Q * C], onehot_r[:, g, :], slotted[:, g, :, :].rearrange("p q c -> p (q c)"),
                                     start=g == 0, stop=g == G - 1)
                last.then_inc(route_mm, 1)

            def slots_transposed(b, k):
                pe.wait_ge(gathered, 16 * GB * (b + 1))
                if KD * b + k:
                    pe.wait_ge(xs_lo, KD * b + k)
                for c in range(GB):
                    last = pe.transpose(bank[6][:, c * P:(c + 1) * P], xg[:, c, k * P:(k + 1) * P], ident[:, :])
                last.then_inc(xsT, 1)

            route(0, 1)
            for k in range(KD):
                slots_transposed(0, k)
            pe.wait_ge(lo0, 4)

            def down(s):
                b, h = s // KH, s % KH
                pe.wait_ge(hid0, s + 1)
                if h == 0 and b >= 2:
                    pe.wait_ge(y_out, b - 1)
                if b % 2 == 0 and b:
                    pe.wait_ge(w2_new, KH * (b // 2 - 1) + h + 1)
                for q in range(GB):
                    out = bank[2 + 2 * (b % 2) + q // 2][:, (q % 2) * D:(q % 2 + 1) * D]
                    last = product(out, at(hid[s % 4], every, slice(q * P, (q + 1) * P)), at(w2, every, h, every),
                                   start=h == 0 and q % 2 == 0, stop=h == KH - 1)
                last.then_inc(down0, 1)

            for b in range(NB0):
                for h in range(KH):
                    s = KH * b + h
                    if s >= 2:
                        pe.wait_ge(gelu0, s - 1)
                    if h == 0:
                        pe.wait_ge(xs_lo, KD * (b + 1))
                    if b % 2 == 0 and b:
                        pe.wait_ge(w1_new, KH * (b // 2 - 1) + h + 1)
                    for k in range(KD):
                        last = product(bank[s % 2][:, :], at(w1, every, k, slice(h * P, (h + 1) * P)),
                                       at(xs[b % 2], every, k, every), start=k == 0, stop=k == KD - 1)
                    last.then_inc(up0, 1)
                    if s >= 2:
                        down(s - 2)
                    if h in (4, 6) and b + 1 < NB0:
                        slots_transposed(b + 1, h // 2 - 2)
                    if h == 6 and b < E - 1:
                        route(b + 1, 1 + 4 * (b + 1))
            down(KH * NB0 - 2)
            down(KH * NB0 - 1)

            def x1_transposed(par, loads, prior, k):
                pe.wait_ge(x1_in[par], loads)
                if prior is not None:
                    pe.wait_ge(*prior)
                for c in range(GB):
                    last = pe.transpose(bank[7][:, c * P:(c + 1) * P], x1_sb[par][:, c, k * P:(k + 1) * P], ident[:, :])
                last.then_inc(x1_t, 1)

            def low_rank(t, par, w):
                for k in range(KD):
                    last = product(bank[7][:, :], at(w, every, k, every), at(x1s[par], every, k, every),
                                   start=k == 0, stop=k == KD - 1)
                last.then_inc(u_mm, 1)

            def prepare(t, par, pair, h):
                if h == 3:
                    x1_transposed(par, 16 * (pair + 1), (u_ev, 2 * t) if not (isinstance(t, int) and t == 0) else None, 0)
                if h == 4:
                    x1_transposed(par, 16 * (pair + 1), (x1_act, KD * t + 1), 1)
                if h == 5:
                    pe.wait_ge(x1_lo, KD * (t + 1))
                    low_rank(t, par, ag)
                if h == 6:
                    pe.wait_ge(u_ev, 2 * t + 1)
                    low_rank(t, par, au)

            def half(w, b, u, x, out, h, done):
                hc = slice(h * P, (h + 1) * P)
                for k in range(KD):
                    product(out, at(w, every, k, hc), at(x, every, k, every), start=k == 0, stop=False)
                product(out, at(b, every, 0, hc), at(u, every, every), start=False, stop=True).then_inc(done, 1)

            def down1_(s, h, t, first):
                pe.wait_ge(hid1_s, s + 1)
                if h == 0 and not first:
                    pe.wait_ge(out_ev, KD * t)
                for k in range(KD):
                    product(bank[4 + k][:, :], at(wd, every, h, slice(k * P, (k + 1) * P)), at(hid1[h % 4], every, every),
                            start=h == 0, stop=False)
                product(bank[6][:, :], at(ad, every, h, every), at(hid1[h % 4], every, every),
                        start=h == 0, stop=h == KH - 1).then_inc(down1, 1)

            def finish(t):
                pe.wait_ge(v_lo, t + 1)
                for k in range(KD):
                    last = product(bank[4 + k][:, :], at(bd, every, 0, slice(k * P, (k + 1) * P)), at(vs, every, every),
                                   start=False, stop=True)
                last.then_inc(acc1, 1)

            def steps1(t, par, pair, first, last):
                for h in range(KH):
                    s = KH * t + h
                    if not (first and h < 2):
                        pe.wait_ge(silu1, s - 1)
                        pe.wait_ge(prod1, s - 1)
                    if h == 0:
                        pe.wait_ge(u_lo, 2 * (t + 1))
                    half(wg, bg, ug[par], x1s[par], bank[h % 2][:, :], h, gate1)
                    if h == 2 and not first:
                        finish(t - 1)
                    half(wu, bu, uu[par], x1s[par], bank[2 + h % 2][:, :], h, up1)
                    if h >= 2:
                        down1_(s - 2, h - 2, t, first)
                    elif not first:
                        down1_(s - 2, KH - 2 + h, t - 1, False)
                    if not last:
                        prepare(t + 1, 1 - par, pair + par, h)

            pe.wait_ge(lo1, NP1)
            for h in range(3, 7):
                prepare(0, 0, 0, h)
            pe.wait_ge(y_out, NB0)
            steps1(0, 0, 0, True, False)
            steps1(1, 1, 0, False, False)
            with pe.Fori(1, NB1 // 2 - 1) as i:
                steps1(2 * i, 0, i, False, False)
                steps1(2 * i + 1, 1, i, False, False)
            steps1(NB1 - 2, 0, NB1 // 2 - 1, False, False)
            steps1(NB1 - 1, 1, NB1 // 2 - 1, False, True)
            down1_(KH * NB1 - 2, KH - 2, NB1 - 1, False)
            down1_(KH * NB1 - 1, KH - 1, NB1 - 1, False)
            finish(NB1 - 1)


def kernel(**inputs):
    import concourse.bacc as _bacc
    from concourse import mybir as _mybir
    from concourse.bass_utils import run_bass_kernel_spmd as _run

    a = {k: np.asarray(v) for k, v in inputs.items()}
    arrays = {
        "x": a["x"].reshape(TOK, D),
        "itok": a["itok_B_0_7"],
        "itok_by_place": a["itok_B_0_7"].reshape(G, 4).T,
        "L0_cond_weights": a["L0_cond_weights"],
        "L0_ffn_Wg": a["L0_ffn_Wg"], "L0_ffn_bg": a["L0_ffn_bg"],
        "L0_ffn_W1": a["L0_ffn_W1"], "L0_ffn_W2": a["L0_ffn_W2"],
        "L1_cond_Wg": a["L1_cond_Wg"], "L1_cond_Wu": a["L1_cond_Wu"],
        "wdT": a["L1_cond_Wd"].T,
        "ag_all": a["L1_cond_Ag"].transpose(1, 0, 2).reshape(D, P),
        "au_all": a["L1_cond_Au"].transpose(1, 0, 2).reshape(D, P),
        "ad_all": a["L1_cond_Ad"].transpose(1, 0, 2).reshape(HID, P),
        "bg_all": a["L1_cond_Bg"].reshape(P, HID),
        "bu_all": a["L1_cond_Bu"].reshape(P, HID),
        "bdT": a["L1_cond_Bd"].reshape(P, D).T,
        "wfT": a["L1_ffn_weight"].T,
        "L1_ffn_scale_weight": a["L1_ffn_scale_weight"],
        "out_bias_cols": a["L1_ffn_bias"].reshape(KD, P).T,
        **shape_constants(),
    }
    arrays = {f"in_{n}": np.ascontiguousarray(v) for n, v in arrays.items()}
    nc = _bacc.Bacc("TRN2", target_bir_lowering=False, num_devices=1)
    args = {n[3:]: nc.dram_tensor(n, v.shape, _mybir.dt.from_np(v.dtype), kind="ExternalInput").ap()
            for n, v in arrays.items()}
    outT = nc.dram_tensor("outT", (KD, P, TOK), _mybir.dt.float32, kind="ExternalOutput").ap()
    adaln_moe_lora(nc, args, outT)
    r = _run(nc, [arrays], core_ids=[0])
    got = r.results[0]["outT"].reshape(D, TOK)
    return np.ascontiguousarray(got.T).reshape(a["x"].shape)
```

```python
import concourse.bass as bass
from concourse import mybir
from contextlib import ExitStack
import numpy as np

P = 128
TOK, D, HID = 4096, 256, 1024
G = TOK // P
E, CAP = 4, 1024
Q = CAP // P
KD, KH = D // P, HID // P
BT = 512
GB = BT // P
NB0, NB1 = E * CAP // BT, TOK // BT
NAD = 8
C = 6
SB = BT // 32
MAGIC = 12582912.0
LOG2E, LN2_HI, LN2_LO = 1.4426950408889634, 0.693145751953125, 1.4286068203094173e-06
EXP_C = [1 / 5040, 1 / 720, 1 / 120, 1 / 24, 1 / 6, 0.5, 1.0]
SEARCH_STEPS = 15
SEARCH_BODY = 5


F_COLS = {"ident": P, "gate_w": KD * 32, "subj_w": NAD * 32}
F2_COLS = {"cols": 3, "iota": P, "before": P, "restart": 2 * E * G, "behind": E * G, "gate_b": E,
           "scale": D, "out_bias": KD}
I_COLS = {"subj": G, "sample": TOK // 32, "steps": 3}


def shape_constants():
    p = np.arange(P)
    restart = np.ones((P, 2 * E, G), np.float32)
    restart[:, :, 0] = 0.0
    return {
        "ident": np.eye(P, dtype=np.float32),
        "cols": np.stack([p, TOK + p, p // 16], 1).astype(np.float32),
        "iota": np.broadcast_to(np.arange(P, dtype=np.float32), (P, P)),
        "before": (p[:, None] < p[None, :]).astype(np.float32),
        "restart": restart.reshape(P, 2 * E * G),
        "steps": np.broadcast_to(np.array([1, 2, 3], np.int32) << 28, (P, 3)),
        "behind": np.broadcast_to(np.repeat(np.arange(E - 1, -1, -1, dtype=np.float32), G), (P, E * G)),
    }


def adaln_moe_lora(nc, A, outT):
    f32, f32r, bf16 = mybir.dt.float32, mybir.dt.float32r, mybir.dt.bfloat16
    i32, u32 = mybir.dt.int32, mybir.dt.uint32
    ALU, ACT, AX = mybir.AluOpType, mybir.ActivationFunctionType, mybir.AxisListType

    flat_rows = nc.dram_tensor("flat_rows", (TOK + P, D), f32).ap()
    x1_rows = nc.dram_tensor("x1_rows", (TOK + P, D), f32).ap()

    ctx = ExitStack()
    with ctx:
        cursor = [(nc.sbuf_base + 63) // 64 * 64]

        def sb(name, shape, dt):
            t = nc.alloc_sbuf_tensor_at(name, shape, dt, offset=cursor[0])
            cursor[0] += (int(np.prod(shape[1:])) * (2 if dt == bf16 else 4) + 31) // 32 * 32
            assert cursor[0] <= nc.sbuf_usable_end, (name, cursor[0])
            return t

        def two(name, shape):
            return sb(name + "_hi", shape, f32r), sb(name + "_lo", shape, f32r)

        def sem(name):
            return ctx.enter_context(nc.semaphore(name))

        def packed(name, widths, dt):
            t, at, views = sb(name, [P, sum(widths.values())], dt), 0, {}
            for n, w in widths.items():
                views[n] = t[:, at:at + w]
                at += w
            return t, views

        pack_f, vf = packed("pack_f", F_COLS, f32)
        pack_f2, vf2 = packed("pack_f2", F2_COLS, f32)
        pack_i, vi = packed("pack_i", I_COLS, i32)
        ident, iota, before, restart = vf["ident"], vf2["iota"], vf2["before"], vf2["restart"]
        cols, out_bias, gate_b, wf_scale = vf2["cols"], vf2["out_bias"], vf2["gate_b"], vf2["scale"]
        gate_w = vf["gate_w"].rearrange("p (k e) -> p k e", k=KD)
        subj_w = vf["subj_w"].rearrange("p (a d) -> p a d", a=NAD)
        behind = vf2["behind"].rearrange("p (e g) -> p e g", e=E)
        steps = vi["steps"].bitcast(u32)
        iota_b = sb("iota_b", [P, P], bf16)
        warm = sb("warm", [P, 1], f32)
        adapter_mask = sb("adapter_mask", [P, TOK // 32], f32)
        slot_row = sb("slot_row", [P, E, Q], i32)
        slot_p = sb("slot_p", [P, E, Q], f32)
        layer1_at = cursor[0]
        wg, wu = two("wg", [P, KD, HID]), two("wu", [P, KD, HID])
        wd = two("wd", [P, KH, D])
        ag, au = two("ag", [P, KD, P]), two("au", [P, KD, P])
        bg, bu = two("bg", [P, 1, HID]), two("bu", [P, 1, HID])
        ad, bd = two("ad", [P, KH, P]), two("bd", [P, 1, D])
        work_at = cursor[0]

        cursor[0] = layer1_at
        x_sb = sb("x_sb", [P, G, D], f32)
        mix = sb("mix", [P, G, P], f32)
        mix_row = sb("mix_row", [P, G, 32], f32)
        subj_f = sb("subj_f", [P, G], f32)
        subj_is = sb("subj_is", [P, NAD, G], i32)
        zT = sb("zT", [P, BT], f32)
        z = sb("z", [P, G, E], f32)
        zeros = sb("zeros", [P, D], f32)
        flat_st = [sb(f"flat_st{i}", [P, GB, D], f32) for i in range(4)]
        assert cursor[0] <= work_at

        cursor[0] = work_at
        w1, w2 = two("w1", [P, KD, HID]), two("w2", [P, KH, D])
        w1_raw, w2_raw = sb("w1_raw", [P, KD, HID], f32), sb("w2_raw", [P, KH, D], f32)
        pos_r, pos_q = sb("pos_r", [P, E, G], bf16), sb("pos_q", [P, E, G], bf16)
        vals = sb("vals", [P, E, G, C], bf16)
        onehot_q = sb("onehot_q", [P, G, Q], bf16)
        onehot_at = cursor[0]
        onehot_r = sb("onehot_r", [P, G, P], bf16)
        slotted = sb("slotted", [P, G, Q, C], bf16)
        routed = sb("routed", [P, Q, C], f32)
        route_t = sb("route_t", [P, 3, Q], f32)
        late_at = cursor[0]
        xg = sb("xg", [P, GB, D], f32)
        xs = [two(f"xs{i}", [P, KD, BT]) for i in range(2)]
        hid = [two(f"hid{i}", [P, BT]) for i in range(4)]
        hf = [sb(f"hf{i}", [P, BT], f32) for i in range(2)]
        y_sb = [sb(f"y_sb{i}", [P, GB, D], f32) for i in range(2)]
        top_at = cursor[0]
        raw = {n: sb("raw_" + n, s, f32) for n, s in (
            ("bg", [P, 1, HID]), ("bu", [P, 1, HID]), ("ad", [P, KH, P]))}

        cursor[0] = work_at
        xT = [sb(f"xT{i}", [P, KD, BT], f32) for i in range(8)]
        cursor[0] = onehot_at
        wdT = sb("wdT", [P, KD, HID], f32)
        assert cursor[0] <= late_at
        cursor[0] = late_at
        raw |= {n: sb("raw_" + n, s, f32) for n, s in (
            ("wg", [P, KD, HID]), ("wu", [P, KD, HID]), ("wd", [P, KH, D]), ("ag", [P, KD, P]), ("au", [P, KD, P]),
            ("bd", [P, 1, D]))}
        bdT = sb("bdT", [P, KD, P], f32)
        wfT = sb("wfT", [P, KD, D], f32)
        wfT_s = sb("wfT_s", [P, KD, D], f32)
        before_b, ones_b = sb("before_b", [P, P], bf16), sb("ones_b", [P, P], bf16)
        logit = sb("logit", [P, E, G], f32)
        rank = sb("rank", [P, E, G], f32)
        t_eg = [sb(f"t_eg{i}", [P, E, G], f32) for i in range(3)]
        t_g = [sb(f"t_g{i}", [P, G], f32) for i in range(8)]
        prob, score = sb("prob", [P, E, G], f32), sb("score", [P, E, G], f32)
        prob_rest = sb("prob_rest", [P, E, G], f32)
        thr = sb("thr", [P, E], f32)
        cand = sb("cand", [P, E, 3], f32)
        passed = sb("passed", [P, E, 3, G], bf16)
        passed_n = sb("passed_n", [P, E, 3], bf16)
        kept = sb("kept", [P, E, 4], f32)
        above = sb("above", [P, 2, E, G], bf16)
        incl = sb("incl", [P, 2, E, G], f32)
        prefix = sb("prefix", [P, 2, E, G], f32)
        need = sb("need", [P, E], f32)
        pos_i = [sb(f"pos_i{i}", [P, E, G], i32) for i in range(2)]
        assert cursor[0] <= top_at, (cursor[0], top_at)

        cursor[0] = work_at
        x1_sb = [sb(f"x1_sb{i}", [P, GB, D], f32) for i in range(2)]
        x1T = [sb(f"x1T{i}", [P, KD, BT], f32) for i in range(2)]
        x1s = [two(f"x1s{i}", [P, KD, BT]) for i in range(2)]
        ug, uu = [two(f"ug{i}", [P, BT]) for i in range(2)], [two(f"uu{i}", [P, BT]) for i in range(2)]
        um = [sb(f"um{i}", [P, BT], f32) for i in range(2)]
        vm = sb("vm", [P, BT], f32)
        vs = two("vs", [P, BT])
        hid1 = [two(f"hid1_{i}", [P, BT]) for i in range(4)]
        act1 = [sb(f"act1_{i}", [P, BT], f32) for i in range(2)]
        prod = [sb(f"prod{i}", [P, BT], f32) for i in range(2)]
        out_sb = [sb(f"out_sb{i}", [P, KD, BT], f32) for i in range(2)]

        bank = [ctx.enter_context(nc.psum_tensor(f"bank{i}", [P, BT], f32)) for i in range(8)]

        pack_in, pack2_in = sem("pack_in"), sem("pack2_in")
        xT_in = [sem(f"xT_in{i}") for i in range(8)]
        x_in = [sem(f"x_in{i}") for i in range(8)]
        fold_w_in, raw0_in, raw1_in = sem("fold_w_in"), sem("raw0_in"), sem("raw1_in")
        flat_out = [sem(f"flat_out{i}") for i in range(4)]
        x1_init, spare_out = sem("x1_init"), sem("spare_out")
        zeroed = sem("zeroed")
        z_mm, z_ev, z_tr, z_in = sem("z_mm"), sem("z_ev"), sem("z_tr"), sem("z_in")
        mix_rows, mixed = sem("mix_rows"), sem("mixed")
        logit_mm, logit_in = sem("logit_mm"), sem("logit_in")
        fold_in, item_mm, item_ev = sem("fold_in"), sem("item_mm"), sem("item_ev")
        hi0, lo0 = sem("hi0"), sem("lo0")
        hi1, lo1 = sem("hi1"), sem("lo1")
        hi1_late, lo1_late = sem("hi1_late"), sem("lo1_late")
        chain = sem("chain")
        asked, counted = sem("asked"), sem("counted")
        ranks_in, ranked = sem("ranks_in"), sem("ranked")
        prob_in, vals_own, vals_in = sem("prob_in"), sem("vals_own"), sem("vals_in")
        route_in, route_mm, route_out = sem("route_in"), sem("route_mm"), sem("route_out")
        gathered, scattered = [sem(f"gathered{i}") for i in range(GB)], sem("scattered")
        up0, gelu0, hi_0, hid0, down0 = sem("up0"), sem("gelu0"), sem("hi_0"), sem("hid0"), sem("down0")
        xsT, xs_hi, xs_lo = sem("xsT"), sem("xs_hi"), sem("xs_lo")
        y_out = sem("y_out")
        nw_hi, w1_new, w2_new = sem("nw_hi"), sem("w1_new"), sem("w2_new")
        x1_in = [sem(f"x1_in{i}") for i in range(2)]
        x1_t, x1_act, x1_lo = sem("x1_t"), sem("x1_act"), sem("x1_lo")
        u_mm, u_ev, u_hi, u_lo = sem("u_mm"), sem("u_ev"), sem("u_hi"), sem("u_lo")
        gate1, up1, silu1, prod1, phi1, hid1_s, down1 = (sem("gate1"), sem("up1"), sem("silu1"), sem("prod1"),
                                                         sem("phi1"), sem("hid1"), sem("down1"))
        v_ev, v_hi, v_lo = sem("v_ev"), sem("v_hi"), sem("v_lo")
        acc1, out_ev = sem("acc1"), sem("out_ev")
        out_done = [sem(f"out_done{i}") for i in range(2)]

        SPLITS = [(raw[n], w) for n, w in (("wg", wg), ("wu", wu), ("ag", ag), ("au", au), ("wd", wd), ("bd", bd))]
        NPLAIN = 4
        LATE_SPLITS = [(raw[n], w) for n, w in (("bg", bg), ("bu", bu), ("ad", ad))]

        def pieces(t):
            n = max(1, 1024 // t.shape[2])
            return [slice(a, min(a + n, t.shape[1])) for a in range(0, t.shape[1], n)]

        NP1 = sum(len(pieces(r)) for r, _ in SPLITS)
        ITEMS = G + KH // 2 + 1
        ROWS_FIRST = 14

        block = ctx.enter_context(nc.Block())

        @block.sync
        def _(sp):
            xT_v = A["xT"].rearrange("(k p) n -> p k n", p=P)
            x_v = A["x"].rearrange("(g p) d -> p g d", p=P)
            sp.dma_start(pack_i[:, :], A["pack_i"]).then_inc(pack_in, 16)
            sp.dma_start(pack_f[:, :], A["pack_f"]).then_inc(pack_in, 16)
            for i in range(8):
                sp.dma_start(xT[i][:, :, :], xT_v[:, :, i * BT:(i + 1) * BT]).then_inc(xT_in[i], 16)
                if i == 0:
                    sp.dma_start(pack_f2[:, :], A["pack_f2"]).then_inc(pack2_in, 16)
            sp.wait_ge(xT_in[3], 16)
            for i in range(8):
                sp.dma_start(x_sb[:, i * GB:(i + 1) * GB, :], x_v[:, i * GB:(i + 1) * GB, :]).then_inc(x_in[i], 16)
            sp.wait_ge(x_in[1], 16)
            for dst, src in ((wfT, A["wfT"]), (wdT, A["wdT"]), (bdT, A["bdT"])):
                sp.dma_start(dst[:, :, :], src.rearrange("(k p) n -> p k n", p=P)).then_inc(fold_w_in, 16)

            def load_expert(e, done):
                sp.dma_start(w1_raw[:, :, :], A["L0_ffn_W1"][e].rearrange("(k p) n -> p k n", p=P)).then_inc(done, 16)
                sp.dma_start(w2_raw[:, :, :], A["L0_ffn_W2"][e].rearrange("(k p) n -> p k n", p=P)).then_inc(done, 16)

            sp.wait_ge(x_in[4], 16)
            load_expert(0, raw0_in)
            sp.wait_ge(zeroed, 2)
            for rows in (x1_rows, flat_rows):
                sp.dma_start(rows[TOK:TOK + P, :], zeros[:, :]).then_inc(spare_out, 16)
            sp.wait_ge(x_in[7], 16)
            for n, src in (("wg", A["L1_cond_Wg"]), ("wu", A["L1_cond_Wu"]), ("ag", A["ag_all"]), ("au", A["au_all"])):
                sp.dma_start(raw[n][:, :, :], src.rearrange("(k p) n -> p k n", p=P)).then_inc(raw1_in, 16)
            flat_v = flat_rows[0:TOK].rearrange("(g p) d -> p g d", p=P)
            for i in range(8):
                sp.wait_ge(item_ev, (i + 1) * GB)
                sp.dma_start(flat_v[:, i * GB:(i + 1) * GB, :], flat_st[i % 4][:, :, :]).then_inc(flat_out[i % 4], 16)
            for n, src in (("bg", A["bg_all"]), ("bu", A["bu_all"]), ("ad", A["ad_all"])):
                sp.dma_start(raw[n][:, :, :], src.rearrange("(k p) n -> p k n", p=P)).then_inc(raw1_in, 16)
            for i in range(4):
                r = slice(i * TOK // 4, (i + 1) * TOK // 4)
                sp.dma_start(x1_rows[r, :], A["x"][r, :]).then_inc(x1_init, 16)
            for e in range(1, E):
                if e == 1:
                    sp.wait_ge(lo0, 4)
                else:
                    sp.wait_ge(w1_new, KH * (e - 1))
                    sp.wait_ge(w2_new, KH * (e - 1))
                load_expert(e, raw0_in)
            x1_b = x1_rows[0:TOK].rearrange("(t g p) d -> t p g d", p=P, g=GB)
            out_v = outT.rearrange("k p (t n) -> t p k n", n=BT)
            sp.wait_ge(scattered, 16 * GB * NB0)
            for t in range(2):
                sp.dma_start(x1_sb[t][:, :, :], x1_b[t]).then_inc(x1_in[t], 16)
            for t in range(NB1):
                if t + 2 < NB1:
                    sp.wait_ge(x1_t, KD * (t + 1))
                    sp.dma_start(x1_sb[t % 2][:, :, :], x1_b[t + 2]).then_inc(x1_in[t % 2], 16)
                sp.wait_ge(out_ev, KD * (t + 1))
                sp.dma_start(out_v[t], out_sb[t % 2][:, :, :]).then_inc(out_done[t % 2], 16)
            for i in range(2):
                sp.wait_ge(out_done[i], 16 * NB1 // 2)

        @block.gpsimd
        def _(pool):
            pool.memset(zeros[:, :], 0.0).then_inc(zeroed, 1)
            pool.memset(mix[:, :, :], 0.0).then_inc(zeroed, 1)
            n = 0
            for r, (hi, lo) in ((w1_raw, w1), (w2_raw, w2)):
                for a in pieces(r):
                    n += 1
                    pool.wait_ge(hi0, n)
                    pool.tensor_tensor(lo[:, a, :], r[:, a, :], hi[:, a, :].bitcast(f32), ALU.subtract).then_inc(lo0, 1)
            pool.wait_ge(prob_in, 1)
            pool.tensor_copy(vals[:, :, :, 0], cols[:, 0:1].unsqueeze(2).to_broadcast([P, E, G]))
            pool.tensor_copy(vals[:, :, :, 1], iota[:, 0:G].unsqueeze(1).to_broadcast([P, E, G]))
            pool.memset(vals[:, :, :, 2], 1.0)
            pool.tensor_copy(vals[:, :, :, 3], prob[:, :, :]).then_inc(vals_own, 1)
            pool.wait_ge(vals_own, 1)
            pool.tensor_tensor(prob_rest[:, :, :], prob[:, :, :], vals[:, :, :, 3], ALU.subtract).then_inc(vals_own, 1)
            pool.wait_ge(vals_own, 2)
            pool.tensor_copy(vals[:, :, :, 4], prob_rest[:, :, :]).then_inc(vals_own, 1)
            pool.wait_ge(vals_own, 3)
            pool.tensor_tensor(vals[:, :, :, 5], prob_rest[:, :, :], vals[:, :, :, 4], ALU.subtract).then_inc(vals_in, 1)
            n = 0
            for r, (hi, lo) in SPLITS:
                for a in pieces(r):
                    n += 1
                    pool.wait_ge(hi1, n)
                    pool.tensor_tensor(lo[:, a, :], r[:, a, :], hi[:, a, :].bitcast(f32), ALU.subtract).then_inc(lo1, 1)

            def gather(b):
                e, half = b // 2, b % 2
                pool.wait_ge(route_out, e + 1)
                if b:
                    pool.wait_ge(xsT, KD * b)
                for q in range(GB):
                    pool.indirect_dma_start(
                        out=xg[:, q, :], out_offset=None, in_=flat_rows[:, :],
                        in_offset=bass.IndirectOffsetOnAxis(ap=slot_row[:, e, half * GB + q:half * GB + q + 1], axis=0),
                    ).then_inc(gathered[q], 16)

            def scatter(b):
                e, half = b // 2, b % 2
                pool.wait_ge(y_out, b + 1)
                if b:
                    pool.wait_ge(scattered, 16 * GB * b)
                for q in range(GB):
                    pool.indirect_dma_start(
                        out=x1_rows[:, :],
                        out_offset=bass.IndirectOffsetOnAxis(ap=slot_row[:, e, half * GB + q:half * GB + q + 1], axis=0),
                        in_=y_sb[half][:, q, :], in_offset=None, compute_op=ALU.add).then_inc(scattered, 16)

            for i in range(4):
                pool.wait_ge(flat_out[i], 32)
            pool.wait_ge(spare_out, 32)
            pool.wait_ge(lo1, NP1)
            gather(0)
            for b in range(NB0):
                if b + 1 < NB0:
                    gather(b + 1)
                if b == 1:
                    pool.wait_ge(x1_init, 64)
                if b:
                    scatter(b - 1)
            scatter(NB0 - 1)

        @block.scalar
        def _(act):
            for h in range(2):
                act.wait_ge(z_mm, h + 1)
                if h:
                    act.wait_ge(z_tr, 1)
                act.activation(zT[:, :], bank[2 + 5 * h][:, :], ACT.Copy).then_inc(z_ev, 1)
                if h == 0:
                    act.wait_ge(mix_rows, 1)
                    act.wait_ge(zeroed, 2)
                    for s in range(4):
                        r = slice(32 * s, 32 * s + 32)
                        act.activation(mix[r, :, r], mix_row[r, :, :], ACT.Copy).then_inc(mixed, 1)
            for n in range(ITEMS):
                act.wait_ge(item_mm, n + 1)
                src = bank[n % 4]
                if n < G:
                    if n >= 4 * GB and n % GB == 0:
                        act.wait_ge(flat_out[n // GB % 4], 16 * (n // GB // 4))
                    last = act.activation(flat_st[n // GB % 4][:, n % GB, :], src[:, 0:D], ACT.Copy)
                elif n < ITEMS - 1:
                    last = act.activation(raw["wd"][:, 2 * (n - G):2 * (n - G) + 2, :],
                                          src[:, :].rearrange("p (a n) -> p a n", a=2), ACT.Copy)
                else:
                    last = act.activation(raw["bd"][:, 0, :], src[:, 0:D], ACT.Copy)
                last.then_inc(item_ev, 1)
                if n == ROWS_FIRST:
                    act.wait_ge(raw0_in, 32)
                    for r, (hi, lo) in ((w1_raw, w1), (w2_raw, w2)):
                        for a in pieces(r):
                            act.activation(hi[:, a, :], r[:, a, :], ACT.Copy).then_inc(hi0, 1)
            for i in range(4):
                act.wait_ge(flat_out[i], 32)
            act.wait_ge(spare_out, 32)
            act.wait_ge(raw1_in, 64)
            act.wait_ge(item_ev, ITEMS)
            for r, (hi, lo) in SPLITS:
                for a in pieces(r):
                    act.activation(hi[:, a, :], r[:, a, :], ACT.Copy).then_inc(hi1, 1)
            act.wait_ge(raw1_in, 112)
            for r, (hi, lo) in LATE_SPLITS:
                act.activation(hi[:, :, :], r[:, :, :], ACT.Copy).then_inc(hi1_late, 1)
            act.activation(warm[:, :], cols[:, 0:1], ACT.Gelu)

            def slots_hi(b, k):
                act.wait_ge(xsT, KD * b + k + 1)
                act.activation(xs[b % 2][0][:, k, :], bank[6][:, :], ACT.Copy).then_inc(xs_hi, 1)

            def rows_of_y(b):
                e = b // 2
                act.wait_ge(down0, KH * (b + 1))
                if b >= 2:
                    act.wait_ge(scattered, 16 * GB * (b - 1))
                for q in range(GB):
                    src = bank[2 + 2 * (b % 2) + q // 2][:, (q % 2) * D:(q % 2 + 1) * D]
                    last = act.activation(y_sb[b % 2][:, q, :], src, ACT.Copy,
                                          scale=slot_p[:, e, (b % 2) * GB + q:(b % 2) * GB + q + 1])
                last.then_inc(y_out, 1)

            for k in range(KD):
                slots_hi(0, k)
            for b in range(NB0):
                for h in range(KH):
                    s = KH * b + h
                    act.wait_ge(up0, s + 1)
                    if s >= 2:
                        act.wait_ge(hid0, s - 1)
                    act.activation(hf[s % 2][:, :], bank[s % 2][:, :], ACT.Gelu).then_inc(gelu0, 1)
                    if h == 1 and b:
                        rows_of_y(b - 1)
                    if h in (5, 7) and b + 1 < NB0:
                        slots_hi(b + 1, h // 2 - 2)
                    if b % 2 and b < NB0 - 1:
                        if h == 0:
                            act.wait_ge(raw0_in, 32 * (b // 2 + 2))
                        hc = slice(h * P, (h + 1) * P)
                        act.activation(w1[0][:, :, hc], w1_raw[:, :, hc], ACT.Copy).then_inc(nw_hi, 1)
                        if h >= 2:
                            act.wait_ge(down0, s - 1)
                            act.activation(w2[0][:, h - 2, :], w2_raw[:, h - 2, :], ACT.Copy).then_inc(nw_hi, 1)
                    if b and b % 2 == 0 and h < 2:
                        act.wait_ge(down0, s - 1)
                        act.activation(w2[0][:, KH - 2 + h, :], w2_raw[:, KH - 2 + h, :], ACT.Copy).then_inc(nw_hi, 1)
            rows_of_y(NB0 - 1)
            act.activation(warm[:, :], cols[:, 0:1], ACT.Silu)

            def x1_parts(par, n, k):
                act.wait_ge(x1_t, n)
                act.activation(x1T[par][:, k, :], bank[7][:, :], ACT.Copy)
                act.activation(x1s[par][0][:, k, :], bank[7][:, :], ACT.Copy).then_inc(x1_act, 1)

            def steps1(t, par, first, last):
                for h in range(KH):
                    s = KH * t + h
                    act.wait_ge(gate1, s + 1)
                    if not (first and h < 2):
                        act.wait_ge(prod1, s - 1)
                    act.activation(act1[h % 2][:, :], bank[h % 2][:, :], ACT.Silu).then_inc(silu1, 1)
                    if h in (3, 4) and not last:
                        if h == 3 and not first:
                            act.wait_ge(out_ev, KD * t)
                        x1_parts(1 - par, KD * (t + 1) + h - 2, h - 3)

            for k in range(KD):
                x1_parts(0, k + 1, k)
            steps1(0, 0, True, False)
            steps1(1, 1, False, False)
            with act.Fori(1, NB1 // 2 - 1) as i:
                steps1(2 * i, 0, False, False)
                steps1(2 * i + 1, 1, False, False)
            steps1(NB1 - 2, 0, False, False)
            steps1(NB1 - 1, 1, False, True)

        @block.vector
        def _(dve):
            n_chain = 0

            def link(ins):
                nonlocal n_chain
                n_chain += 1
                ins.then_inc(chain, 1)
                dve.wait_ge(chain, n_chain)

            def over(ap, n):
                return ap.unsqueeze(len(ap.shape)).to_broadcast(list(ap.shape) + [n])

            vf2_iota8 = iota[:, 0:NAD]
            dve.wait_ge(pack_in, 32)
            dve.wait_ge(pack2_in, 16)
            link(dve.tensor_copy(subj_f[:, :], vi["subj"]))
            link(dve.tensor_tensor(subj_is[:, :, :], subj_f[:, :].unsqueeze(1).to_broadcast([P, NAD, G]),
                                   over(vf2_iota8, G), ALU.is_equal))
            link(dve.memset(mix_row[:, :, :], 0.0))
            for a in range(NAD):
                link(dve.copy_predicated(mix_row[:, :, :], over(subj_is[:, a, :], 32),
                                         subj_w[:, a, :].unsqueeze(1).to_broadcast([P, G, 32])))
            dve.memset(ones_b[:, :], 1.0).then_inc(mix_rows, 1)
            dve.tensor_copy(iota_b[:, :], iota)
            dve.tensor_copy(before_b[:, :], before)
            link(dve.tensor_copy(adapter_mask[:, :], vi["sample"]))
            link(dve.tensor_scalar(adapter_mask[:, :], adapter_mask[:, :], cols[:, 2:3], None, ALU.is_equal))
            link(dve.memset(kept[:, :, 3], 0.0))
            link(dve.memset(thr[:, :], 0.0))
            for s in range(2):
                dve.wait_ge(z_tr, s + 1)
                dst = z[:, s * 16:(s + 1) * 16, :].rearrange("p (j c) e -> p j c e", j=4)
                src = bank[3][:, :].rearrange("p (c j r) -> p j c r", c=4, j=4)[:, :, :, 0:E]
                dve.tensor_copy(dst, src).then_inc(z_in, 1)
            for s in range(2):
                dve.wait_ge(logit_mm, s + 1)
                src = bank[5 + s][:, 0:G // 2 * E].rearrange("p (g e) -> p e g", e=E)
                link(dve.tensor_tensor(logit[:, :, s * 16:(s + 1) * 16], src, over(gate_b, G // 2), ALU.add))
            link(dve.tensor_copy(rank[:, :, :], behind))
            for d in range(1, E):
                link(dve.tensor_tensor(t_eg[0][:, 0:E - d, :], logit[:, 0:E - d, :], logit[:, d:E, :], ALU.is_ge))
                link(dve.tensor_tensor(rank[:, d:E, :], rank[:, d:E, :], t_eg[0][:, 0:E - d, :], ALU.add))
                link(dve.tensor_tensor(rank[:, 0:E - d, :], rank[:, 0:E - d, :], t_eg[0][:, 0:E - d, :], ALU.subtract))
            m1, m2, neg, n_f, r_, t_, p1, p2 = t_g
            dve.tensor_reduce(m1[:, :], logit[:, :, :].rearrange("p e g -> p g e"), AX.X, ALU.max)
            link(dve.scalar_tensor_tensor(t_eg[0][:, :, :], rank[:, :, :], 1.0, logit[:, :, :], ALU.is_equal, ALU.mult))
            link(dve.tensor_reduce(m2[:, :], t_eg[0][:, :, :].rearrange("p e g -> p g e"), AX.X, ALU.add))
            link(dve.tensor_tensor(neg[:, :], m2[:, :], m1[:, :], ALU.subtract))
            link(dve.tensor_scalar(neg[:, :], neg[:, :], -87.0, None, ALU.max))
            link(dve.tensor_scalar(n_f[:, :], neg[:, :], LOG2E, MAGIC + 127.0, ALU.mult, ALU.add))
            link(dve.tensor_scalar(p1[:, :], n_f[:, :], -(MAGIC + 127.0), None, ALU.add))
            link(dve.scalar_tensor_tensor(r_[:, :], p1[:, :], -LN2_HI, neg[:, :], ALU.mult, ALU.add))
            link(dve.scalar_tensor_tensor(r_[:, :], p1[:, :], -LN2_LO, r_[:, :], ALU.mult, ALU.add))
            link(dve.tensor_scalar(t_[:, :], r_[:, :], EXP_C[0], None, ALU.mult))
            for c in EXP_C[1:]:
                link(dve.scalar_tensor_tensor(t_[:, :], t_[:, :], c, r_[:, :], ALU.add, ALU.mult))
            link(dve.tensor_scalar(t_[:, :], t_[:, :], 1.0, None, ALU.add))
            link(dve.tensor_scalar(n_f[:, :].bitcast(u32), n_f[:, :].bitcast(u32), 23, None, ALU.logical_shift_left))
            link(dve.tensor_tensor(t_[:, :], t_[:, :], n_f[:, :], ALU.mult))
            link(dve.tensor_scalar(m1[:, :], t_[:, :], 1.0, None, ALU.add))
            link(dve.reciprocal(p1[:, :], m1[:, :]))
            link(dve.tensor_tensor(p2[:, :], t_[:, :], p1[:, :], ALU.mult))
            for i, p_ in ((0, p1), (1, p2)):
                link(dve.scalar_tensor_tensor(t_eg[i][:, :, :], rank[:, :, :], float(i),
                                              p_[:, :].unsqueeze(1).to_broadcast([P, E, G]), ALU.is_equal, ALU.mult))
            dve.tensor_tensor(prob[:, :, :], t_eg[0][:, :, :], t_eg[1][:, :, :], ALU.add).then_inc(prob_in, 1)
            dve.wait_ge(prob_in, 1)
            link(dve.tensor_scalar(t_eg[2][:, :, :], rank[:, :, :], 2.0, None, ALU.is_ge))
            link(dve.tensor_tensor(score[:, :, :], prob[:, :, :], t_eg[2][:, :, :], ALU.subtract))

            dve.wait_ge(fold_w_in, 48)
            dve.tensor_tensor(wfT_s[:, :, :], wfT[:, :, :], wf_scale.unsqueeze(1).to_broadcast([P, KD, D]),
                              ALU.mult).then_inc(fold_in, 1)
            base, OWN = n_chain, 6
            with dve.Fori(0, SEARCH_STEPS // SEARCH_BODY) as it:
                for j in range(SEARCH_BODY):
                    def own(ins, k):
                        ins.then_inc(chain, 1)
                        if k:
                            dve.wait_ge(chain, it * (OWN * SEARCH_BODY) + (base + OWN * j + k))
                    own(dve.tensor_tensor(cand[:, :, :].bitcast(u32), over(thr[:, :].bitcast(u32), 3),
                                          steps.unsqueeze(1).to_broadcast([P, E, 3]), ALU.bitwise_or), 1)
                    own(dve.tensor_tensor(passed[:, :, :, :], score[:, :, :].unsqueeze(2).to_broadcast([P, E, 3, G]),
                                          over(cand[:, :, :], G), ALU.is_ge), 2)
                    with nc.allow_low_precision("counts up to 32"):
                        dve.tensor_reduce(passed_n[:, :, :], passed[:, :, :, :], AX.X, ALU.add).then_inc(asked, 1)
                    own(dve.tensor_copy(kept[:, :, 3], thr[:, :]), 0)
                    own(dve.tensor_scalar(steps, steps, 2, None, ALU.logical_shift_right), 0)
                    dve.wait_ge(counted, it * SEARCH_BODY + (j + 1))
                    own(dve.scalar_tensor_tensor(kept[:, :, 0:3], bank[4][:, 0:3 * E].rearrange("p (e j) -> p e j", j=3),
                                                 float(CAP), cand[:, :, :], ALU.is_ge, ALU.mult), 5)
                    own(dve.tensor_reduce(thr[:, :], kept[:, :, :], AX.X, ALU.max), 6)
            n_chain = base + SEARCH_STEPS * OWN

            thr_b = over(thr[:, :], G)
            dve.tensor_tensor(above[:, 0, :, :], score[:, :, :], thr_b, ALU.is_gt)
            dve.tensor_tensor(above[:, 1, :, :], score[:, :, :], thr_b, ALU.is_equal).then_inc(ranks_in, 1)
            dve.wait_ge(ranked, 2)
            flat2 = lambda t: t[:, :, :, :].rearrange("p a e g -> p (a e g)")
            link(dve.tensor_tensor_scan(flat2(incl), restart, bank[6][:, 0:2 * E * G], 0.0, ALU.mult, ALU.add))
            link(dve.tensor_tensor(flat2(prefix), flat2(incl), bank[6][:, 0:2 * E * G], ALU.subtract))
            link(dve.tensor_tensor(flat2(prefix), flat2(prefix), bank[5][:, 0:2 * E * G], ALU.add))
            link(dve.tensor_scalar(need[:, :], incl[:, 0, :, G - 1], -1.0, float(CAP), ALU.mult, ALU.add))
            need_b = over(need[:, :], G)
            link(dve.tensor_tensor(t_eg[0][:, :, :], prefix[:, 1, :, :], need_b, ALU.is_lt))
            link(dve.tensor_tensor(t_eg[0][:, :, :], t_eg[0][:, :, :], above[:, 1, :, :], ALU.mult))
            link(dve.tensor_tensor(t_eg[0][:, :, :], t_eg[0][:, :, :], above[:, 0, :, :], ALU.add))
            link(dve.tensor_tensor(t_eg[1][:, :, :], prefix[:, 1, :, :], need_b, ALU.min))
            link(dve.tensor_tensor(pos_i[0][:, :, :], t_eg[1][:, :, :], prefix[:, 0, :, :], ALU.add))
            link(dve.tensor_scalar(pos_i[1][:, :, :], pos_i[0][:, :, :], 7, None, ALU.logical_shift_right))
            link(dve.tensor_scalar(pos_i[0][:, :, :], pos_i[0][:, :, :], 127, None, ALU.bitwise_and))
            dve.tensor_copy(pos_r[:, :, :], pos_i[0][:, :, :])
            link(dve.tensor_scalar(t_eg[0][:, :, :], t_eg[0][:, :, :], -64.0, 64.0, ALU.mult, ALU.add))
            link(dve.tensor_tensor(pos_q[:, :, :], pos_i[1][:, :, :], t_eg[0][:, :, :], ALU.add))
            dve.wait_ge(vals_in, 1)

            def route_make(e, part, parts=1):
                g = slice(part * G // parts, (part + 1) * G // parts)
                n = G // parts
                link(dve.tensor_tensor(onehot_q[:, g, :], over(pos_q[:, e, g], Q),
                                       iota_b[:, 0:Q].unsqueeze(1).to_broadcast([P, n, Q]), ALU.is_equal))
                dve.tensor_tensor(slotted[:, g, :, :], over(onehot_q[:, g, :], C),
                                  vals[:, e, g, :].unsqueeze(2).to_broadcast([P, n, Q, C]), ALU.mult)
                dve.tensor_tensor(onehot_r[:, g, :], over(pos_r[:, e, g], P),
                                  iota_b[:, :].unsqueeze(1).to_broadcast([P, n, P]), ALU.is_equal).then_inc(route_in, 1)

            def route_read(e):
                dve.wait_ge(route_mm, e + 1)
                link(dve.tensor_copy(routed[:, :, :], bank[7][:, 0:Q * C].rearrange("p (q c) -> p q c", c=C)))
                link(dve.scalar_tensor_tensor(route_t[:, 0, :], routed[:, :, 1], float(P), routed[:, :, 0], ALU.mult, ALU.add))
                link(dve.tensor_scalar(route_t[:, 1, :], routed[:, :, 2], -1.0, 1.0, ALU.mult, ALU.add))
                link(dve.scalar_tensor_tensor(slot_row[:, e, :], route_t[:, 1, :], cols[:, 1:2], route_t[:, 0, :], ALU.mult, ALU.add))
                link(dve.tensor_tensor(route_t[:, 2, :], routed[:, :, 3], routed[:, :, 4], ALU.add))
                dve.tensor_tensor(slot_p[:, e, :], route_t[:, 2, :], routed[:, :, 5], ALU.add).then_inc(route_out, 1)

            route_make(0, 0)
            route_read(0)

            def slots_lo(b, k):
                dve.wait_ge(xs_hi, KD * b + k + 1)
                hi, lo = xs[b % 2]
                dve.tensor_tensor(lo[:, k, :], bank[6][:, :], hi[:, k, :].bitcast(f32), ALU.subtract).then_inc(xs_lo, 1)

            n_new = 0

            def new_lo(lo, hi, r, done):
                nonlocal n_new
                n_new += 1
                dve.wait_ge(nw_hi, n_new)
                dve.tensor_tensor(lo, r, hi.bitcast(f32), ALU.subtract).then_inc(done, 1)

            for k in range(KD):
                slots_lo(0, k)
            for b in range(NB0):
                for h in range(KH):
                    s = KH * b + h
                    hi, lo = hid[s % 4]
                    dve.wait_ge(gelu0, s + 1)
                    if s >= 4:
                        dve.wait_ge(down0, s - 3)
                    dve.tensor_copy(hi[:, :], hf[s % 2][:, :]).then_inc(hi_0, 1)
                    dve.wait_ge(hi_0, s + 1)
                    dve.tensor_tensor(lo[:, :], hf[s % 2][:, :], hi[:, :].bitcast(f32), ALU.subtract).then_inc(hid0, 1)
                    if h in (5, 7) and b + 1 < NB0:
                        slots_lo(b + 1, h // 2 - 2)
                    if b < E - 1 and 1 <= h < 5:
                        if h == 1 and b:
                            dve.wait_ge(route_mm, b + 1)
                        route_make(b + 1, h - 1, 4)
                    if b < E - 1 and h == 7:
                        route_read(b + 1)
                    if b == 0 and h in (0, 5, 6):
                        j = (0, 5, 6).index(h)
                        dve.wait_ge(hi1_late, j + 1)
                        r, (hi_, lo_) = LATE_SPLITS[j]
                        dve.tensor_tensor(lo_[:, :, :], r[:, :, :], hi_[:, :, :].bitcast(f32), ALU.subtract).then_inc(lo1_late, 1)
                    if b % 2 and b < NB0 - 1:
                        hc = slice(h * P, (h + 1) * P)
                        new_lo(w1[1][:, :, hc], w1[0][:, :, hc], w1_raw[:, :, hc], w1_new)
                        if h >= 2:
                            new_lo(w2[1][:, h - 2, :], w2[0][:, h - 2, :], w2_raw[:, h - 2, :], w2_new)
                    if b and b % 2 == 0 and h < 2:
                        new_lo(w2[1][:, KH - 2 + h, :], w2[0][:, KH - 2 + h, :], w2_raw[:, KH - 2 + h, :], w2_new)

            def masked(dst, src, t):
                m = adapter_mask[:, bass.ds(t * SB, SB)]
                return dve.tensor_tensor(dst[:, :].rearrange("p (s n) -> p s n", n=32),
                                         src[:, :].rearrange("p (s n) -> p s n", n=32), over(m, 32), ALU.mult)

            def x1_low(par, n, k):
                dve.wait_ge(x1_act, n)
                dve.tensor_tensor(x1s[par][1][:, k, :], x1T[par][:, k, :], x1s[par][0][:, k, :].bitcast(f32),
                                  ALU.subtract).then_inc(x1_lo, 1)

            def u_parts(t, par, j, parts):
                n = 2 * t + j + 1
                dve.wait_ge(u_mm, n)
                masked(um[j], bank[7], t).then_inc(u_ev, 1)
                dve.wait_ge(u_ev, n)
                dve.tensor_copy(parts[0][:, :], um[j][:, :]).then_inc(u_hi, 1)
                dve.wait_ge(u_hi, n)
                dve.tensor_tensor(parts[1][:, :], um[j][:, :], parts[0][:, :].bitcast(f32), ALU.subtract).then_inc(u_lo, 1)

            def finish_v(t):
                dve.wait_ge(down1, KH * (t + 1))
                masked(vm, bank[6], t).then_inc(v_ev, 1)
                dve.wait_ge(v_ev, t + 1)
                dve.tensor_copy(vs[0][:, :], vm[:, :]).then_inc(v_hi, 1)
                dve.wait_ge(v_hi, t + 1)
                dve.tensor_tensor(vs[1][:, :], vm[:, :], vs[0][:, :].bitcast(f32), ALU.subtract).then_inc(v_lo, 1)

            def finish_out(t, par, wait_store):
                dve.wait_ge(acc1, t + 1)
                if wait_store is not None:
                    dve.wait_ge(out_done[par], wait_store)
                for k in range(KD):
                    dve.scalar_tensor_tensor(out_sb[par][:, k, :], bank[4 + k][:, :], out_bias[:, k:k + 1],
                                             x1T[par][:, k, :], ALU.add, ALU.add).then_inc(out_ev, 1)

            def steps1(t, par, pair, first, last):
                for h in range(KH):
                    s = KH * t + h
                    if h == 2 and not first:
                        before_ = pair if par else pair - 1
                        prior = None if isinstance(pair, int) and before_ <= 0 else 16 * before_
                        finish_out(t - 1, 1 - par, prior)
                    dve.wait_ge(up1, s + 1)
                    dve.wait_ge(silu1, s + 1)
                    if not (first and h < 2):
                        dve.wait_ge(hid1_s, s - 1)
                    dve.tensor_tensor(prod[h % 2][:, :], bank[2 + h % 2][:, :], act1[h % 2][:, :], ALU.mult).then_inc(prod1, 1)
                    dve.wait_ge(prod1, s + 1)
                    if not (first and h < 4):
                        dve.wait_ge(down1, s - 3)
                    dve.tensor_copy(hid1[h % 4][0][:, :], prod[h % 2][:, :]).then_inc(phi1, 1)
                    dve.wait_ge(phi1, s + 1)
                    dve.tensor_tensor(hid1[h % 4][1][:, :], prod[h % 2][:, :], hid1[h % 4][0][:, :].bitcast(f32),
                                      ALU.subtract).then_inc(hid1_s, 1)
                    if h == 1 and not first:
                        finish_v(t - 1)
                    if h in (3, 4) and not last:
                        x1_low(1 - par, KD * (t + 1) + h - 2, h - 3)
                    if h == 5 and not last:
                        u_parts(t + 1, 1 - par, 0, ug[1 - par])
                    if h == 6 and not last:
                        u_parts(t + 1, 1 - par, 1, uu[1 - par])

            for k in range(KD):
                x1_low(0, k + 1, k)
            u_parts(0, 0, 0, ug[0])
            u_parts(0, 0, 1, uu[0])
            steps1(0, 0, 0, True, False)
            steps1(1, 1, 0, False, False)
            with dve.Fori(1, NB1 // 2 - 1) as i:
                steps1(2 * i, 0, i, False, False)
                steps1(2 * i + 1, 1, i, False, False)
            steps1(NB1 - 2, 0, NB1 // 2 - 1, False, False)
            steps1(NB1 - 1, 1, NB1 // 2 - 1, False, True)
            finish_v(NB1 - 1)
            finish_out(NB1 - 1, 1, 16 * (NB1 // 2 - 1))

        @block.tensor
        def _(pe):
            def product(out, lhs, rhs, start, stop):
                (lh, ll), (rh, rl) = lhs, rhs
                pe.matmul(out, lh, rh, start=start, stop=False, skip_group_check=True)
                pe.matmul(out, lh, rl, start=False, stop=False, skip_group_check=True)
                return pe.matmul(out, ll, rh, start=False, stop=stop, skip_group_check=True)

            def at(parts, *index):
                return tuple(p[index] for p in parts)

            every = slice(None)
            pe.wait_ge(pack_in, 32)

            def z_by_token(h):
                pe.wait_ge(z_ev, h + 1)
                if h:
                    pe.wait_ge(z_in, 1)
                for c in range(GB):
                    last = pe.transpose(bank[3][:, c * P:(c + 1) * P], zT[:, c * P:(c + 1) * P], ident)
                last.then_inc(z_tr, 1)

            def logits(h):
                pe.wait_ge(mixed, 4)
                pe.wait_ge(z_in, h + 1)
                for g in range(G // 2):
                    last = pe.matmul(bank[5 + h][:, g * E:(g + 1) * E], mix[:, h * 16 + g, :], z[:, h * 16 + g, :],
                                     start=True, stop=True)
                last.then_inc(logit_mm, 1)

            for i in range(8):
                pe.wait_ge(xT_in[i], 16)
                j = i % 4
                for k in range(KD):
                    last = pe.matmul(bank[2 + 5 * (i // 4)][32 * j:32 * j + 32, :], gate_w[:, k, :], xT[i][:, k, :],
                                     start=k == 0, stop=k == KD - 1, tile_position=(0, 32 * j))
                if j == 3:
                    last.then_inc(z_mm, 1)
                if i == 5:
                    z_by_token(0)
            logits(0)
            z_by_token(1)
            logits(1)

            def item(n):
                if n == 0:
                    pe.wait_ge(z_in, 2)
                if n >= 4:
                    pe.wait_ge(item_ev, n - 3)
                out = bank[n % 4]
                if n < G:
                    if n % GB == 0:
                        pe.wait_ge(x_in[n // GB], 16)
                    last = pe.matmul(out[:, 0:D], mix[:, n, :], x_sb[:, n, :], start=True, stop=True)
                elif n < ITEMS - 1:
                    if n == G:
                        pe.wait_ge(fold_in, 1)
                    for a in range(2):
                        h = 2 * (n - G) + a
                        for k in range(KD):
                            last = pe.matmul(out[:, a * D:(a + 1) * D], wdT[:, k, h * P:(h + 1) * P], wfT_s[:, k, :],
                                             start=k == 0, stop=k == KD - 1)
                else:
                    for k in range(KD):
                        last = pe.matmul(out[:, 0:D], bdT[:, k, :], wfT_s[:, k, :], start=k == 0, stop=k == KD - 1)
                last.then_inc(item_mm, 1)

            for n in range(ROWS_FIRST):
                item(n)
            n = ROWS_FIRST
            for i in range(SEARCH_STEPS):
                pe.wait_ge(asked, i + 1)
                pe.matmul(bank[4][:, 0:3 * E], ones_b[:, :], passed_n[:, :, :].rearrange("p e j -> p (e j)"),
                          start=True, stop=True).then_inc(counted, 1)
                for _ in range(2 if n < G else 1):
                    if n < ITEMS:
                        item(n)
                        n += 1
            assert n == ITEMS
            pe.wait_ge(ranks_in, 1)
            marks = above[:, :, :, :].rearrange("p a e g -> p (a e g)")
            pe.matmul(bank[5][:, 0:2 * E * G], before_b[:, :], marks, start=True, stop=True).then_inc(ranked, 1)
            pe.matmul(bank[6][:, 0:2 * E * G], ones_b[:, :], marks, start=True, stop=True).then_inc(ranked, 1)

            def route(e, n):
                pe.wait_ge(route_in, n)
                if e:
                    pe.wait_ge(route_out, e)
                for g in range(G):
                    last = pe.matmul(bank[7][:, 0:Q * C], onehot_r[:, g, :], slotted[:, g, :, :].rearrange("p q c -> p (q c)"),
                                     start=g == 0, stop=g == G - 1)
                last.then_inc(route_mm, 1)

            def slots_transposed(b, k):
                if KD * b + k:
                    pe.wait_ge(xs_lo, KD * b + k)
                for c in range(GB):
                    pe.wait_ge(gathered[c], 16 * (b + 1))
                    last = pe.transpose(bank[6][:, c * P:(c + 1) * P], xg[:, c, k * P:(k + 1) * P], ident)
                last.then_inc(xsT, 1)

            route(0, 1)
            for k in range(KD):
                slots_transposed(0, k)
            pe.wait_ge(lo0, 4)

            def down(s):
                b, h = s // KH, s % KH
                pe.wait_ge(hid0, s + 1)
                if h == 0 and b >= 2:
                    pe.wait_ge(y_out, b - 1)
                if b % 2 == 0 and b:
                    pe.wait_ge(w2_new, KH * (b // 2 - 1) + h + 1)
                for q in range(GB):
                    out = bank[2 + 2 * (b % 2) + q // 2][:, (q % 2) * D:(q % 2 + 1) * D]
                    last = product(out, at(hid[s % 4], every, slice(q * P, (q + 1) * P)), at(w2, every, h, every),
                                   start=h == 0 and q % 2 == 0, stop=h == KH - 1)
                last.then_inc(down0, 1)

            for b in range(NB0):
                for h in range(KH):
                    s = KH * b + h
                    if s >= 2:
                        pe.wait_ge(gelu0, s - 1)
                    if h == 0:
                        pe.wait_ge(xs_lo, KD * (b + 1))
                    if b % 2 == 0 and b:
                        pe.wait_ge(w1_new, KH * (b // 2 - 1) + h + 1)
                    for k in range(KD):
                        last = product(bank[s % 2][:, :], at(w1, every, k, slice(h * P, (h + 1) * P)),
                                       at(xs[b % 2], every, k, every), start=k == 0, stop=k == KD - 1)
                    last.then_inc(up0, 1)
                    if s >= 2:
                        down(s - 2)
                    if h in (4, 6) and b + 1 < NB0:
                        slots_transposed(b + 1, h // 2 - 2)
                    if h == 6 and b < E - 1:
                        route(b + 1, 1 + 4 * (b + 1))
            down(KH * NB0 - 2)
            down(KH * NB0 - 1)

            def x1_transposed(par, loads, prior, k):
                pe.wait_ge(x1_in[par], loads)
                if prior is not None:
                    pe.wait_ge(*prior)
                for c in range(GB):
                    last = pe.transpose(bank[7][:, c * P:(c + 1) * P], x1_sb[par][:, c, k * P:(k + 1) * P], ident)
                last.then_inc(x1_t, 1)

            def low_rank(t, par, w):
                for k in range(KD):
                    last = product(bank[7][:, :], at(w, every, k, every), at(x1s[par], every, k, every),
                                   start=k == 0, stop=k == KD - 1)
                last.then_inc(u_mm, 1)

            def prepare(t, par, pair, h):
                if h == 3:
                    x1_transposed(par, 16 * (pair + 1), (u_ev, 2 * t) if not (isinstance(t, int) and t == 0) else None, 0)
                if h == 4:
                    x1_transposed(par, 16 * (pair + 1), (x1_act, KD * t + 1), 1)
                if h == 5:
                    pe.wait_ge(x1_lo, KD * (t + 1))
                    low_rank(t, par, ag)
                if h == 6:
                    pe.wait_ge(u_ev, 2 * t + 1)
                    low_rank(t, par, au)

            def half(w, b, u, x, out, h, done):
                hc = slice(h * P, (h + 1) * P)
                for k in range(KD):
                    product(out, at(w, every, k, hc), at(x, every, k, every), start=k == 0, stop=False)
                product(out, at(b, every, 0, hc), at(u, every, every), start=False, stop=True).then_inc(done, 1)

            def down1_(s, h, t, first):
                pe.wait_ge(hid1_s, s + 1)
                if h == 0 and not first:
                    pe.wait_ge(out_ev, KD * t)
                for k in range(KD):
                    product(bank[4 + k][:, :], at(wd, every, h, slice(k * P, (k + 1) * P)), at(hid1[h % 4], every, every),
                            start=h == 0, stop=False)
                product(bank[6][:, :], at(ad, every, h, every), at(hid1[h % 4], every, every),
                        start=h == 0, stop=h == KH - 1).then_inc(down1, 1)

            def finish(t):
                pe.wait_ge(v_lo, t + 1)
                for k in range(KD):
                    last = product(bank[4 + k][:, :], at(bd, every, 0, slice(k * P, (k + 1) * P)), at(vs, every, every),
                                   start=False, stop=True)
                last.then_inc(acc1, 1)

            def steps1(t, par, pair, first, last):
                for h in range(KH):
                    s = KH * t + h
                    if not (first and h < 2):
                        pe.wait_ge(silu1, s - 1)
                        pe.wait_ge(prod1, s - 1)
                    if h == 0:
                        pe.wait_ge(u_lo, 2 * (t + 1))
                    half(wg, bg, ug[par], x1s[par], bank[h % 2][:, :], h, gate1)
                    if h == 2 and not first:
                        finish(t - 1)
                    half(wu, bu, uu[par], x1s[par], bank[2 + h % 2][:, :], h, up1)
                    if h >= 2:
                        down1_(s - 2, h - 2, t, first)
                    elif not first:
                        down1_(s - 2, KH - 2 + h, t - 1, False)
                    if not last:
                        prepare(t + 1, 1 - par, pair + par, h)

            pe.wait_ge(lo1, NP1)
            pe.wait_ge(lo1_late, 3)
            for h in range(3, 7):
                prepare(0, 0, 0, h)
            pe.wait_ge(y_out, NB0)
            steps1(0, 0, 0, True, False)
            steps1(1, 1, 0, False, False)
            with pe.Fori(1, NB1 // 2 - 1) as i:
                steps1(2 * i, 0, i, False, False)
                steps1(2 * i + 1, 1, i, False, False)
            steps1(NB1 - 2, 0, NB1 // 2 - 1, False, False)
            steps1(NB1 - 1, 1, NB1 // 2 - 1, False, True)
            down1_(KH * NB1 - 2, KH - 2, NB1 - 1, False)
            down1_(KH * NB1 - 1, KH - 1, NB1 - 1, False)
            finish(NB1 - 1)


def kernel(**inputs):
    import concourse.bacc as _bacc
    from concourse import mybir as _mybir
    from concourse.bass_utils import run_bass_kernel_spmd as _run

    a = {k: np.asarray(v) for k, v in inputs.items()}
    consts = shape_constants()
    itok = a["itok_B_0_7"]
    wide = lambda v: np.broadcast_to(v, (P, v.size))
    gate_w = np.zeros((P, KD, 32), a["L0_ffn_Wg"].dtype)
    gate_w[:, :, :E] = a["L0_ffn_Wg"].reshape(KD, P, E).transpose(1, 0, 2)
    small = {
        **consts,
        "gate_w": gate_w.reshape(P, KD * 32),
        "subj_w": np.tile(a["L0_cond_weights"].transpose(1, 0, 2).reshape(32, NAD * 32), (4, 1)),
        "subj": np.repeat(itok.reshape(G, 4).T, 32, axis=0),
        "sample": wide(itok), "gate_b": wide(a["L0_ffn_bg"]), "scale": wide(a["L1_ffn_scale_weight"]),
        "out_bias": a["L1_ffn_bias"].reshape(KD, P).T,
    }
    arrays = {
        **{n: np.concatenate([small[c] for c in names], 1)
           for n, names in (("pack_f", F_COLS), ("pack_f2", F2_COLS), ("pack_i", I_COLS))},
        "x": a["x"].reshape(TOK, D),
        "xT": a["x"].reshape(TOK, D).T,
        "L0_ffn_W1": a["L0_ffn_W1"], "L0_ffn_W2": a["L0_ffn_W2"],
        "L1_cond_Wg": a["L1_cond_Wg"], "L1_cond_Wu": a["L1_cond_Wu"],
        "wdT": a["L1_cond_Wd"].T,
        "ag_all": a["L1_cond_Ag"].transpose(1, 0, 2).reshape(D, P),
        "au_all": a["L1_cond_Au"].transpose(1, 0, 2).reshape(D, P),
        "ad_all": a["L1_cond_Ad"].transpose(1, 0, 2).reshape(HID, P),
        "bg_all": a["L1_cond_Bg"].reshape(P, HID),
        "bu_all": a["L1_cond_Bu"].reshape(P, HID),
        "bdT": a["L1_cond_Bd"].reshape(P, D).T,
        "wfT": a["L1_ffn_weight"].T,
    }
    arrays = {f"in_{n}": np.ascontiguousarray(v) for n, v in arrays.items()}
    nc = _bacc.Bacc("TRN2", target_bir_lowering=False, num_devices=1)
    args = {n[3:]: nc.dram_tensor(n, v.shape, _mybir.dt.from_np(v.dtype), kind="ExternalInput").ap()
            for n, v in arrays.items()}
    outT = nc.dram_tensor("outT", (KD, P, TOK), _mybir.dt.float32, kind="ExternalOutput").ap()
    adaln_moe_lora(nc, args, outT)
    r = _run(nc, [arrays], core_ids=[0])
    got = r.results[0]["outT"].reshape(D, TOK)
    return np.ascontiguousarray(got.T).reshape(a["x"].shape)
```

```python
import concourse.bass as bass
from concourse import mybir
from contextlib import ExitStack
import numpy as np

P = 128
TOK, D, HID = 4096, 256, 1024
G = TOK // P
E, CAP = 4, 1024
Q = CAP // P
KD, KH = D // P, HID // P
BT = 512
GB = BT // P
NB0, NB1 = E * CAP // BT, TOK // BT
NAD = 8
C = 6
SB = BT // 32
MAGIC = 12582912.0
LOG2E, LN2_HI, LN2_LO = 1.4426950408889634, 0.693145751953125, 1.4286068203094173e-06
EXP_C = [1 / 5040, 1 / 720, 1 / 120, 1 / 24, 1 / 6, 0.5, 1.0]
SEARCH_STEPS = 15
SEARCH_BODY = 5


F_COLS = {"ident": P, "gate_w": KD * 32, "subj_w": NAD * 32}
F2_COLS = {"cols": 3, "iota": P, "before": P, "restart": 2 * E * G, "behind": E * G, "gate_b": E,
           "scale": D, "out_bias": KD}
I_COLS = {"subj": G, "sample": TOK // 32, "steps": 3}


def shape_constants():
    p = np.arange(P)
    restart = np.ones((P, 2 * E, G), np.float32)
    restart[:, :, 0] = 0.0
    return {
        "ident": np.eye(P, dtype=np.float32),
        "cols": np.stack([p, TOK + p, p // 16], 1).astype(np.float32),
        "iota": np.broadcast_to(np.arange(P, dtype=np.float32), (P, P)),
        "before": (p[:, None] < p[None, :]).astype(np.float32),
        "restart": restart.reshape(P, 2 * E * G),
        "steps": np.broadcast_to(np.array([1, 2, 3], np.int32) << 28, (P, 3)),
        "behind": np.broadcast_to(np.repeat(np.arange(E - 1, -1, -1, dtype=np.float32), G), (P, E * G)),
    }


def adaln_moe_lora(nc, A, outT):
    f32, f32r, bf16 = mybir.dt.float32, mybir.dt.float32r, mybir.dt.bfloat16
    i32, u32 = mybir.dt.int32, mybir.dt.uint32
    ALU, ACT, AX = mybir.AluOpType, mybir.ActivationFunctionType, mybir.AxisListType

    flat_rows = nc.dram_tensor("flat_rows", (TOK + P, D), f32).ap()
    x1_rows = nc.dram_tensor("x1_rows", (TOK + P, D), f32).ap()

    ctx = ExitStack()
    with ctx:
        cursor = [(nc.sbuf_base + 63) // 64 * 64]

        def sb(name, shape, dt):
            t = nc.alloc_sbuf_tensor_at(name, shape, dt, offset=cursor[0])
            cursor[0] += (int(np.prod(shape[1:])) * (2 if dt == bf16 else 4) + 31) // 32 * 32
            assert cursor[0] <= nc.sbuf_usable_end, (name, cursor[0])
            return t

        def two(name, shape):
            return sb(name + "_hi", shape, f32r), sb(name + "_lo", shape, f32r)

        def sem(name):
            return ctx.enter_context(nc.semaphore(name))

        def packed(name, widths, dt):
            t, at, views = sb(name, [P, sum(widths.values())], dt), 0, {}
            for n, w in widths.items():
                views[n] = t[:, at:at + w]
                at += w
            return t, views

        pack_f, vf = packed("pack_f", F_COLS, f32)
        pack_f2, vf2 = packed("pack_f2", F2_COLS, f32)
        pack_i, vi = packed("pack_i", I_COLS, i32)
        ident, iota, before, restart = vf["ident"], vf2["iota"], vf2["before"], vf2["restart"]
        cols, out_bias, gate_b, wf_scale = vf2["cols"], vf2["out_bias"], vf2["gate_b"], vf2["scale"]
        gate_w = vf["gate_w"].rearrange("p (k e) -> p k e", k=KD)
        subj_w = vf["subj_w"].rearrange("p (a d) -> p a d", a=NAD)
        behind = vf2["behind"].rearrange("p (e g) -> p e g", e=E)
        steps = vi["steps"].bitcast(u32)
        iota_b = sb("iota_b", [P, P], bf16)
        ident_r = sb("ident_r", [P, P], f32r)
        warm = sb("warm", [P, 1], f32)
        adapter_mask = sb("adapter_mask", [P, TOK // 32], f32)
        slot_row = sb("slot_row", [P, E, Q], i32)
        slot_p = sb("slot_p", [P, E, Q], f32)
        layer1_at = cursor[0]
        wg, wu = two("wg", [P, KD, HID]), two("wu", [P, KD, HID])
        wd = two("wd", [P, KH, D])
        ag, au = two("ag", [P, KD, P]), two("au", [P, KD, P])
        bg, bu = two("bg", [P, 1, HID]), two("bu", [P, 1, HID])
        ad, bd = two("ad", [P, KH, P]), two("bd", [P, 1, D])
        work_at = cursor[0]

        cursor[0] = layer1_at
        x_sb = sb("x_sb", [P, G, D], f32)
        mix = sb("mix", [P, G, P], f32)
        mix_row = sb("mix_row", [P, G, 32], f32)
        subj_f = sb("subj_f", [P, G], f32)
        subj_is = sb("subj_is", [P, NAD, G], i32)
        zT = sb("zT", [P, BT], f32)
        z = sb("z", [P, G, 32], f32)
        zeros = sb("zeros", [P, D], f32)
        flat_st = [sb(f"flat_st{i}", [P, GB, D], f32) for i in range(4)]
        assert cursor[0] <= work_at

        cursor[0] = work_at
        w1, w2 = two("w1", [P, KD, HID]), two("w2", [P, KH, D])
        w1_raw, w2_raw = sb("w1_raw", [P, KD, HID], f32), sb("w2_raw", [P, KH, D], f32)
        pos_r, pos_q = sb("pos_r", [P, E, G], bf16), sb("pos_q", [P, E, G], bf16)
        vals = sb("vals", [P, E, G, C], bf16)
        onehot_q = sb("onehot_q", [P, G, Q], bf16)
        onehot_at = cursor[0]
        onehot_r = sb("onehot_r", [P, G, P], bf16)
        slotted = sb("slotted", [P, G, Q, C], bf16)
        routed = sb("routed", [P, Q, C], f32)
        route_t = sb("route_t", [P, 3, Q], f32)
        late_at = cursor[0]
        xg = sb("xg", [P, GB, D], f32)
        xs = [two(f"xs{i}", [P, KD, BT]) for i in range(2)]
        hid = [two(f"hid{i}", [P, BT]) for i in range(4)]
        hf = [sb(f"hf{i}", [P, BT], f32) for i in range(2)]
        y_sb = [sb(f"y_sb{i}", [P, GB, D], f32) for i in range(2)]
        top_at = cursor[0]
        raw = {n: sb("raw_" + n, s, f32) for n, s in (
            ("bg", [P, 1, HID]), ("bu", [P, 1, HID]), ("ad", [P, KH, P]))}

        cursor[0] = work_at
        xT = [sb(f"xT{i}", [P, KD, BT], f32) for i in range(8)]
        logitT = xT[0]
        cursor[0] = onehot_at
        wdT = sb("wdT", [P, KD, HID], f32)
        assert cursor[0] <= late_at
        cursor[0] = late_at
        raw |= {n: sb("raw_" + n, s, f32) for n, s in (
            ("wg", [P, KD, HID]), ("wu", [P, KD, HID]), ("wd", [P, KH, D]), ("ag", [P, KD, P]), ("au", [P, KD, P]),
            ("bd", [P, 1, D]))}
        bdT = sb("bdT", [P, KD, P], f32)
        wfT = sb("wfT", [P, KD, D], f32)
        wfT_s = sb("wfT_s", [P, KD, D], f32)
        before_b, ones_b = sb("before_b", [P, P], bf16), sb("ones_b", [P, P], bf16)
        logit = sb("logit", [P, E, G], f32)
        rank = sb("rank", [P, E, G], f32)
        t_eg = [sb(f"t_eg{i}", [P, E, G], f32) for i in range(3)]
        t_g = [sb(f"t_g{i}", [P, G], f32) for i in range(8)]
        prob, score = sb("prob", [P, E, G], f32), sb("score", [P, E, G], f32)
        prob_rest = sb("prob_rest", [P, E, G], f32)
        thr = sb("thr", [P, E], f32)
        cand = sb("cand", [P, E, 3], f32)
        passed = sb("passed", [P, E, 3, G], bf16)
        passed_n = sb("passed_n", [P, E, 3], bf16)
        kept = sb("kept", [P, E, 4], f32)
        above = sb("above", [P, 2, E, G], bf16)
        incl = sb("incl", [P, 2, E, G], f32)
        prefix = sb("prefix", [P, 2, E, G], f32)
        need = sb("need", [P, E], f32)
        pos_i = [sb(f"pos_i{i}", [P, E, G], i32) for i in range(2)]
        assert cursor[0] <= top_at, (cursor[0], top_at)

        cursor[0] = work_at
        x1_sb = [sb(f"x1_sb{i}", [P, GB, D], f32) for i in range(2)]
        x1T = [sb(f"x1T{i}", [P, KD, BT], f32) for i in range(2)]
        x1s = [two(f"x1s{i}", [P, KD, BT]) for i in range(2)]
        ug, uu = [two(f"ug{i}", [P, BT]) for i in range(2)], [two(f"uu{i}", [P, BT]) for i in range(2)]
        um = [sb(f"um{i}", [P, BT], f32) for i in range(2)]
        vm = sb("vm", [P, BT], f32)
        vs = two("vs", [P, BT])
        hid1 = [two(f"hid1_{i}", [P, BT]) for i in range(4)]
        act1 = [sb(f"act1_{i}", [P, BT], f32) for i in range(2)]
        prod = [sb(f"prod{i}", [P, BT], f32) for i in range(2)]
        out_sb = [sb(f"out_sb{i}", [P, KD, BT], f32) for i in range(2)]

        bank = [ctx.enter_context(nc.psum_tensor(f"bank{i}", [P, BT], f32)) for i in range(8)]

        def y_at(b, q):
            if b == NB0 - 1:
                return bank[4 + q][:, 0:D]
            return bank[2 + 2 * (b % 2) + q // 2][:, (q % 2) * D:(q % 2 + 1) * D]

        pack_in, pack2_in = sem("pack_in"), sem("pack2_in")
        xT_in = [sem(f"xT_in{i}") for i in range(8)]
        x_in = [sem(f"x_in{i}") for i in range(8)]
        fold_w_in, raw0_in, raw1_in = sem("fold_w_in"), sem("raw0_in"), sem("raw1_in")
        flat_out = [sem(f"flat_out{i}") for i in range(4)]
        x1_init, spare_out = sem("x1_init"), sem("spare_out")
        zeroed = sem("zeroed")
        z_mm, z_ev, z_tr, z_in = sem("z_mm"), sem("z_ev"), sem("z_tr"), sem("z_in")
        mix_rows, mixed = sem("mix_rows"), sem("mixed")
        logit_mm, logit_ev, logit_tr = sem("logit_mm"), sem("logit_ev"), sem("logit_tr")
        fold_in, item_mm, item_ev = sem("fold_in"), sem("item_mm"), sem("item_ev")
        ident_in = sem("ident_in")
        hi0, lo0 = sem("hi0"), sem("lo0")
        hi1, lo1 = sem("hi1"), sem("lo1")
        hi1_late, lo1_late = sem("hi1_late"), sem("lo1_late")
        chain = sem("chain")
        asked, counted = sem("asked"), sem("counted")
        ranks_in, ranked = sem("ranks_in"), sem("ranked")
        prob_in, vals_own, vals_in = sem("prob_in"), sem("vals_own"), sem("vals_in")
        route_in, route_mm, route_out = sem("route_in"), sem("route_mm"), sem("route_out")
        gathered, scattered = [sem(f"gathered{i}") for i in range(GB)], sem("scattered")
        up0, gelu0, hi_0, hid0, down0 = sem("up0"), sem("gelu0"), sem("hi_0"), sem("hid0"), sem("down0")
        xsT, xs_hi, xs_lo = sem("xsT"), sem("xs_hi"), sem("xs_lo")
        y_out = sem("y_out")
        nw_hi, w1_new, w2_new = sem("nw_hi"), sem("w1_new"), sem("w2_new")
        x1_in = [sem(f"x1_in{i}") for i in range(2)]
        x1_t, x1_act, x1_lo = sem("x1_t"), sem("x1_act"), sem("x1_lo")
        u_mm, u_ev, u_hi, u_lo = sem("u_mm"), sem("u_ev"), sem("u_hi"), sem("u_lo")
        gate1, up1, silu1, prod1, phi1, hid1_s, down1 = (sem("gate1"), sem("up1"), sem("silu1"), sem("prod1"),
                                                         sem("phi1"), sem("hid1"), sem("down1"))
        v_ev, v_hi, v_lo = sem("v_ev"), sem("v_hi"), sem("v_lo")
        acc1, out_ev = sem("acc1"), sem("out_ev")
        out_done = [sem(f"out_done{i}") for i in range(2)]

        SPLITS = [(raw[n], w) for n, w in (("wg", wg), ("wu", wu), ("ag", ag), ("au", au), ("wd", wd), ("bd", bd))]
        NPLAIN = 4
        LATE_SPLITS = [(raw[n], w) for n, w in (("bg", bg), ("bu", bu), ("ad", ad))]

        def pieces(t):
            n = max(1, 1024 // t.shape[2])
            return [slice(a, min(a + n, t.shape[1])) for a in range(0, t.shape[1], n)]

        NP1 = sum(len(pieces(r)) for r, _ in SPLITS)
        ITEMS = G + KH // 2 + 1
        ROWS_BEFORE_SPLITS = 22
        ROWS_FIRST = 12

        WAIT_GATHER, WAIT_ROWS, WAIT_PARTS0, WAIT_X1 = 8, 2, 6, 32

        block = ctx.enter_context(nc.Block())

        @block.sync
        def _(sp):
            xT_v = A["xT"].rearrange("(k p) n -> p k n", p=P)
            x_v = A["x"].rearrange("(g p) d -> p g d", p=P)
            sp.dma_start(pack_i[:, :], A["pack_i"]).then_inc(pack_in, 16)
            sp.dma_start(pack_f[:, :], A["pack_f"]).then_inc(pack_in, 16)
            for i in range(8):
                sp.dma_start(xT[i][:, :, :], xT_v[:, :, i * BT:(i + 1) * BT]).then_inc(xT_in[i], 16)
                if i == 0:
                    sp.dma_start(pack_f2[:, :], A["pack_f2"]).then_inc(pack2_in, 16)
            sp.wait_ge(xT_in[5], 16)
            for i in range(8):
                sp.dma_start(x_sb[:, i * GB:(i + 1) * GB, :], x_v[:, i * GB:(i + 1) * GB, :]).then_inc(x_in[i], 16)
            sp.wait_ge(x_in[5], 16)
            for dst, src in ((wfT, A["wfT"]), (wdT, A["wdT"]), (bdT, A["bdT"])):
                sp.dma_start(dst[:, :, :], src.rearrange("(k p) n -> p k n", p=P)).then_inc(fold_w_in, 16)

            def load_expert(e, done):
                sp.dma_start(w1_raw[:, :, :], A["L0_ffn_W1"][e].rearrange("(k p) n -> p k n", p=P)).then_inc(done, 16)
                sp.dma_start(w2_raw[:, :, :], A["L0_ffn_W2"][e].rearrange("(k p) n -> p k n", p=P)).then_inc(done, 16)

            sp.wait_ge(x_in[7], 16)
            load_expert(0, raw0_in)
            sp.wait_ge(zeroed, 2)
            for rows in (x1_rows, flat_rows):
                sp.dma_start(rows[TOK:TOK + P, :], zeros[:, :]).then_inc(spare_out, 16)
            sp.wait_ge(x_in[7], 16)
            for n, src in (("wg", A["L1_cond_Wg"]), ("wu", A["L1_cond_Wu"]), ("ag", A["ag_all"]), ("au", A["au_all"])):
                sp.dma_start(raw[n][:, :, :], src.rearrange("(k p) n -> p k n", p=P)).then_inc(raw1_in, 16)
            flat_v = flat_rows[0:TOK].rearrange("(g p) d -> p g d", p=P)
            for i in range(8):
                sp.wait_ge(item_ev, (i + 1) * GB)
                sp.dma_start(flat_v[:, i * GB:(i + 1) * GB, :], flat_st[i % 4][:, :, :]).then_inc(flat_out[i % 4], 16)
            for n, src in (("bg", A["bg_all"]), ("bu", A["bu_all"]), ("ad", A["ad_all"])):
                sp.dma_start(raw[n][:, :, :], src.rearrange("(k p) n -> p k n", p=P)).then_inc(raw1_in, 16)
            for e in range(1, E):
                if e == 1:
                    sp.wait_ge(lo0, 4)
                else:
                    sp.wait_ge(w1_new, KH * (e - 1))
                    sp.wait_ge(w2_new, KH * (e - 1))
                load_expert(e, raw0_in)
                if e == 1:
                    sp.wait_ge(gathered[GB - 1], 32)
                    for i in range(4):
                        r = slice(i * TOK // 4, (i + 1) * TOK // 4)
                        sp.dma_start(x1_rows[r, :], A["x"][r, :]).then_inc(x1_init, 16)
            x1_b = x1_rows[0:TOK].rearrange("(t g p) d -> t p g d", p=P, g=GB)
            out_v = outT.rearrange("k p (t n) -> t p k n", n=BT)
            sp.wait_ge(scattered, 16 * GB * NB0)
            for t in range(2):
                sp.dma_start(x1_sb[t][:, :, :], x1_b[t]).then_inc(x1_in[t], 16)
            for t in range(NB1):
                if t + 2 < NB1:
                    sp.wait_ge(x1_t, KD * (t + 1))
                    sp.dma_start(x1_sb[t % 2][:, :, :], x1_b[t + 2]).then_inc(x1_in[t % 2], 16)
                if t < NB1 - 1:
                    sp.wait_ge(out_ev, KD * (t + 1))
                    sp.dma_start(out_v[t], out_sb[t % 2][:, :, :]).then_inc(out_done[t % 2], 16)
            for k in range(KD):
                sp.wait_ge(out_ev, KD * (NB1 - 1) + k + 1)
                sp.dma_start(out_v[NB1 - 1, :, k, :], out_sb[1][:, k, :]).then_inc(out_done[1], 16)
            sp.wait_ge(out_done[0], 16 * NB1 // 2)
            sp.wait_ge(out_done[1], 16 * (NB1 // 2 - 1 + KD))

        @block.gpsimd
        def _(pool):
            pool.memset(zeros[:, :], 0.0).then_inc(zeroed, 1)
            pool.memset(mix[:, :, :], 0.0).then_inc(zeroed, 1)
            pool.wait_ge(fold_w_in, 48)
            pool.wait_ge(pack2_in, 16)
            pool.tensor_tensor(wfT_s[:, :, :], wfT[:, :, :], wf_scale.unsqueeze(1).to_broadcast([P, KD, D]),
                               ALU.mult).then_inc(fold_in, 1)
            n = 0
            for r, (hi, lo) in ((w1_raw, w1), (w2_raw, w2)):
                for a in pieces(r):
                    n += 1
                    pool.wait_ge(hi0, n)
                    pool.tensor_tensor(lo[:, a, :], r[:, a, :], hi[:, a, :].bitcast(f32), ALU.subtract).then_inc(lo0, 1)
            pool.wait_ge(prob_in, 1)
            pool.tensor_copy(vals[:, :, :, 0], cols[:, 0:1].unsqueeze(2).to_broadcast([P, E, G]))
            pool.tensor_copy(vals[:, :, :, 1], iota[:, 0:G].unsqueeze(1).to_broadcast([P, E, G]))
            pool.memset(vals[:, :, :, 2], 1.0)
            pool.tensor_copy(vals[:, :, :, 3], prob[:, :, :]).then_inc(vals_own, 1)
            pool.wait_ge(vals_own, 1)
            pool.tensor_tensor(prob_rest[:, :, :], prob[:, :, :], vals[:, :, :, 3], ALU.subtract).then_inc(vals_own, 1)
            pool.wait_ge(vals_own, 2)
            pool.tensor_copy(vals[:, :, :, 4], prob_rest[:, :, :]).then_inc(vals_own, 1)
            pool.wait_ge(vals_own, 3)
            pool.tensor_tensor(vals[:, :, :, 5], prob_rest[:, :, :], vals[:, :, :, 4], ALU.subtract).then_inc(vals_in, 1)
            n = 0
            for r, (hi, lo) in SPLITS:
                for a in pieces(r):
                    n += 1
                    pool.wait_ge(hi1, n)
                    pool.tensor_tensor(lo[:, a, :], r[:, a, :], hi[:, a, :].bitcast(f32), ALU.subtract).then_inc(lo1, 1)

            def gather(b):
                e, half = b // 2, b % 2
                pool.wait_ge(route_out, e + 1)
                if b:
                    pool.wait_ge(xsT, KD * b)
                for q in range(GB):
                    pool.indirect_dma_start(
                        out=xg[:, q, :], out_offset=None, in_=flat_rows[:, :],
                        in_offset=bass.IndirectOffsetOnAxis(ap=slot_row[:, e, half * GB + q:half * GB + q + 1], axis=0),
                    ).then_inc(gathered[q], 16)

            def scatter(b):
                e, half = b // 2, b % 2
                if b:
                    pool.wait_ge(scattered, 16 * GB * b)
                for q in range(GB):
                    pool.wait_ge(y_out, GB * b + q + 1)
                    pool.indirect_dma_start(
                        out=x1_rows[:, :],
                        out_offset=bass.IndirectOffsetOnAxis(ap=slot_row[:, e, half * GB + q:half * GB + q + 1], axis=0),
                        in_=y_sb[half][:, q, :], in_offset=None, compute_op=ALU.add).then_inc(scattered, 16)

            for i in range(4):
                pool.wait_ge(flat_out[i], 32)
            pool.wait_ge(spare_out, 32)
            pool.wait_ge(lo1, NP1)
            gather(0)
            for b in range(NB0):
                if b + 1 < NB0:
                    gather(b + 1)
                if b == 1:
                    pool.wait_ge(x1_init, 64)
                if b:
                    scatter(b - 1)
            scatter(NB0 - 1)

        @block.scalar
        def _(act):
            act.wait_ge(pack_in, 32)
            act.activation(ident_r[:, :], ident, ACT.Copy).then_inc(ident_in, 1)
            for h in range(2):
                act.wait_ge(z_mm, h + 1)
                if h:
                    act.wait_ge(z_tr, 1)
                act.activation(zT[:, :], bank[2 + 5 * h][:, :], ACT.Copy).then_inc(z_ev, 1)
                if h == 0:
                    act.wait_ge(mix_rows, 1)
                    act.wait_ge(zeroed, 2)
                    for s in range(2):
                        r = slice(32 * s, 32 * s + 32)
                        act.activation(mix[r, :, r], mix_row[r, :, :], ACT.Copy).then_inc(mixed, 1)
            for h in range(2):
                act.wait_ge(logit_mm, h + 1)
                act.activation(logitT[:, h, :], bank[5 + h][:, :], ACT.Copy).then_inc(logit_ev, 1)
            for n in range(ITEMS):
                act.wait_ge(item_mm, n + 1)
                src = bank[n % 4]
                if n < G:
                    if n >= 4 * GB and n % GB == 0:
                        act.wait_ge(flat_out[n // GB % 4], 16 * (n // GB // 4))
                    last = act.activation(flat_st[n // GB % 4][:, n % GB, :], src[:, 0:D], ACT.Copy)
                elif n < ITEMS - 1:
                    last = act.activation(raw["wd"][:, 2 * (n - G):2 * (n - G) + 2, :],
                                          src[:, :].rearrange("p (a n) -> p a n", a=2), ACT.Copy)
                else:
                    last = act.activation(raw["bd"][:, 0, :], src[:, 0:D], ACT.Copy)
                last.then_inc(item_ev, 1)
                if n == ROWS_BEFORE_SPLITS:
                    act.wait_ge(raw0_in, 32)
                    for r, (hi, lo) in ((w1_raw, w1), (w2_raw, w2)):
                        for a in pieces(r):
                            act.activation(hi[:, a, :], r[:, a, :], ACT.Copy).then_inc(hi0, 1)
                if n == G - 1:
                    for i in range(4):
                        act.wait_ge(flat_out[i], 32)
                    act.wait_ge(spare_out, 32)
                    act.wait_ge(raw1_in, 64)
                    for r, (hi, lo) in SPLITS[:NPLAIN]:
                        for a in pieces(r):
                            act.activation(hi[:, a, :], r[:, a, :], ACT.Copy).then_inc(hi1, 1)
            act.wait_ge(item_ev, ITEMS)
            for r, (hi, lo) in SPLITS[NPLAIN:]:
                for a in pieces(r):
                    act.activation(hi[:, a, :], r[:, a, :], ACT.Copy).then_inc(hi1, 1)
            act.wait_ge(raw1_in, 112)
            for r, (hi, lo) in LATE_SPLITS:
                act.activation(hi[:, :, :], r[:, :, :], ACT.Copy).then_inc(hi1_late, 1)
            act.activation(warm[:, :], cols[:, 0:1], ACT.Gelu)

            def slots_hi(b, k, src):
                act.wait_ge(xsT, KD * b + k + 1)
                act.activation(xs[b % 2][0][:, k, :], src[:, :], ACT.Copy).then_inc(xs_hi, 1)

            def rows_of_y(b):
                e = b // 2
                if b >= 2:
                    act.wait_ge(scattered, 16 * GB * (b - 1))
                for q in range(GB):
                    if b == NB0 - 1:
                        act.wait_ge(down0, KH * NB0 - GB + q + 1)
                    elif q == 0:
                        act.wait_ge(down0, KH * (b + 1))
                    act.activation(y_sb[b % 2][:, q, :], y_at(b, q), ACT.Copy,
                                   scale=slot_p[:, e, (b % 2) * GB + q:(b % 2) * GB + q + 1]).then_inc(y_out, 1)

            for k in range(KD):
                slots_hi(0, k, bank[6 + k])
            for b in range(NB0):
                for h in range(KH):
                    s = KH * b + h
                    act.wait_ge(up0, s + 1)
                    if s >= 2:
                        act.wait_ge(hid0, s - 1)
                    act.activation(hf[s % 2][:, :], bank[s % 2][:, :], ACT.Gelu).then_inc(gelu0, 1)
                    if h == 1 and b:
                        rows_of_y(b - 1)
                    if h in (4, 6) and b + 1 < NB0:
                        slots_hi(b + 1, (4, 6).index(h), bank[6])
                    if b % 2 and b < NB0 - 1:
                        if h == 0:
                            act.wait_ge(raw0_in, 32 * (b // 2 + 2))
                        hc = slice(h * P, (h + 1) * P)
                        act.activation(w1[0][:, :, hc], w1_raw[:, :, hc], ACT.Copy).then_inc(nw_hi, 1)
                        if h >= 2:
                            act.wait_ge(down0, s - 1)
                            act.activation(w2[0][:, h - 2, :], w2_raw[:, h - 2, :], ACT.Copy).then_inc(nw_hi, 1)
                    if b and b % 2 == 0 and h < 2:
                        act.wait_ge(down0, s - 1)
                        act.activation(w2[0][:, KH - 2 + h, :], w2_raw[:, KH - 2 + h, :], ACT.Copy).then_inc(nw_hi, 1)
            rows_of_y(NB0 - 1)
            act.activation(warm[:, :], cols[:, 0:1], ACT.Silu)

            def x1_parts(par, n, k):
                act.wait_ge(x1_t, n)
                act.activation(x1T[par][:, k, :], bank[7][:, :], ACT.Copy)
                act.activation(x1s[par][0][:, k, :], bank[7][:, :], ACT.Copy).then_inc(x1_act, 1)

            def steps1(t, par, first, last):
                for h in range(KH):
                    s = KH * t + h
                    act.wait_ge(gate1, s + 1)
                    if not (first and h < 2):
                        act.wait_ge(prod1, s - 1)
                    act.activation(act1[h % 2][:, :], bank[h % 2][:, :], ACT.Silu).then_inc(silu1, 1)
                    if h in (3, 4) and not last:
                        if h == 3 and not first:
                            act.wait_ge(out_ev, KD * t)
                        x1_parts(1 - par, KD * (t + 1) + h - 2, h - 3)

            for k in range(KD):
                act.wait_ge(x1_t, k + 1)
                act.activation(x1s[0][0][:, k, :], bank[4 + k][:, :], ACT.Copy).then_inc(x1_act, 1)
            for k in range(KD):
                act.wait_ge(x1_lo, k + 1)
                act.activation(x1T[0][:, k, :], bank[4 + k][:, :], ACT.Copy)
            steps1(0, 0, True, False)
            steps1(1, 1, False, False)
            with act.Fori(1, NB1 // 2 - 1) as i:
                steps1(2 * i, 0, False, False)
                steps1(2 * i + 1, 1, False, False)
            steps1(NB1 - 2, 0, False, False)
            steps1(NB1 - 1, 1, False, True)

        @block.vector
        def _(dve):
            n_chain = 0

            def link(ins):
                nonlocal n_chain
                n_chain += 1
                ins.then_inc(chain, 1)
                dve.wait_ge(chain, n_chain)

            def over(ap, n):
                return ap.unsqueeze(len(ap.shape)).to_broadcast(list(ap.shape) + [n])

            vf2_iota8 = iota[:, 0:NAD]
            dve.wait_ge(pack_in, 32)
            dve.wait_ge(pack2_in, 16)
            link(dve.tensor_copy(subj_f[:, :], vi["subj"]))
            link(dve.tensor_tensor(subj_is[:, :, :], subj_f[:, :].unsqueeze(1).to_broadcast([P, NAD, G]),
                                   over(vf2_iota8, G), ALU.is_equal))
            link(dve.memset(mix_row[:, :, :], 0.0))
            for a in range(NAD):
                link(dve.copy_predicated(mix_row[:, :, :], over(subj_is[:, a, :], 32),
                                         subj_w[:, a, :].unsqueeze(1).to_broadcast([P, G, 32])))
            dve.memset(ones_b[:, :], 1.0).then_inc(mix_rows, 1)
            dve.wait_ge(zeroed, 2)
            for s in range(2, 4):
                r = slice(32 * s, 32 * s + 32)
                dve.tensor_copy(mix[r, :, r], mix_row[r, :, :]).then_inc(mixed, 1)
            dve.tensor_copy(iota_b[:, :], iota)
            dve.tensor_copy(before_b[:, :], before)
            link(dve.tensor_copy(adapter_mask[:, :], vi["sample"]))
            link(dve.tensor_scalar(adapter_mask[:, :], adapter_mask[:, :], cols[:, 2:3], None, ALU.is_equal))
            link(dve.memset(kept[:, :, 3], 0.0))
            link(dve.memset(thr[:, :], 0.0))
            for s in range(2):
                dve.wait_ge(z_tr, s + 1)
                dst = z[:, s * 16:(s + 1) * 16, :].rearrange("p (j c) r -> p j c r", j=4)
                src = bank[3][:, :].rearrange("p (c j r) -> p j c r", c=4, j=4)
                dve.tensor_copy(dst, src).then_inc(z_in, 1)
            for s in range(2):
                dve.wait_ge(logit_tr, s + 1)
                dst = logit[:, :, s * 16:(s + 1) * 16].rearrange("p e (j c) -> p j c e", j=4)
                src = bank[4 + 3 * s][:, :].rearrange("p (c j r) -> p j c r", c=4, j=4)[:, :, :, 0:E]
                link(dve.tensor_tensor(dst, src, gate_b.unsqueeze(1).unsqueeze(1).to_broadcast([P, 4, 4, E]), ALU.add))
            link(dve.tensor_copy(rank[:, :, :], behind))
            for d in range(1, E):
                link(dve.tensor_tensor(t_eg[0][:, 0:E - d, :], logit[:, 0:E - d, :], logit[:, d:E, :], ALU.is_ge))
                link(dve.tensor_tensor(rank[:, d:E, :], rank[:, d:E, :], t_eg[0][:, 0:E - d, :], ALU.add))
                link(dve.tensor_tensor(rank[:, 0:E - d, :], rank[:, 0:E - d, :], t_eg[0][:, 0:E - d, :], ALU.subtract))
            m1, m2, neg, n_f, r_, t_, p1, p2 = t_g
            dve.tensor_reduce(m1[:, :], logit[:, :, :].rearrange("p e g -> p g e"), AX.X, ALU.max)
            link(dve.scalar_tensor_tensor(t_eg[0][:, :, :], rank[:, :, :], 1.0, logit[:, :, :], ALU.is_equal, ALU.mult))
            link(dve.tensor_reduce(m2[:, :], t_eg[0][:, :, :].rearrange("p e g -> p g e"), AX.X, ALU.add))
            link(dve.tensor_tensor(neg[:, :], m2[:, :], m1[:, :], ALU.subtract))
            link(dve.tensor_scalar(neg[:, :], neg[:, :], -87.0, None, ALU.max))
            link(dve.tensor_scalar(n_f[:, :], neg[:, :], LOG2E, MAGIC + 127.0, ALU.mult, ALU.add))
            link(dve.tensor_scalar(p1[:, :], n_f[:, :], -(MAGIC + 127.0), None, ALU.add))
            link(dve.scalar_tensor_tensor(r_[:, :], p1[:, :], -LN2_HI, neg[:, :], ALU.mult, ALU.add))
            link(dve.scalar_tensor_tensor(r_[:, :], p1[:, :], -LN2_LO, r_[:, :], ALU.mult, ALU.add))
            link(dve.tensor_scalar(t_[:, :], r_[:, :], EXP_C[0], None, ALU.mult))
            for c in EXP_C[1:]:
                link(dve.scalar_tensor_tensor(t_[:, :], t_[:, :], c, r_[:, :], ALU.add, ALU.mult))
            link(dve.tensor_scalar(t_[:, :], t_[:, :], 1.0, None, ALU.add))
            link(dve.tensor_scalar(n_f[:, :].bitcast(u32), n_f[:, :].bitcast(u32), 23, None, ALU.logical_shift_left))
            link(dve.tensor_tensor(t_[:, :], t_[:, :], n_f[:, :], ALU.mult))
            link(dve.tensor_scalar(m1[:, :], t_[:, :], 1.0, None, ALU.add))
            link(dve.reciprocal(p1[:, :], m1[:, :]))
            link(dve.tensor_tensor(p2[:, :], t_[:, :], p1[:, :], ALU.mult))
            for i, p_ in ((0, p1), (1, p2)):
                link(dve.scalar_tensor_tensor(t_eg[i][:, :, :], rank[:, :, :], float(i),
                                              p_[:, :].unsqueeze(1).to_broadcast([P, E, G]), ALU.is_equal, ALU.mult))
            dve.tensor_tensor(prob[:, :, :], t_eg[0][:, :, :], t_eg[1][:, :, :], ALU.add).then_inc(prob_in, 1)
            dve.wait_ge(prob_in, 1)
            link(dve.tensor_scalar(t_eg[2][:, :, :], rank[:, :, :], 2.0, None, ALU.is_ge))
            link(dve.tensor_tensor(score[:, :, :], prob[:, :, :], t_eg[2][:, :, :], ALU.subtract))

            base, OWN = n_chain, 6
            with dve.Fori(0, SEARCH_STEPS // SEARCH_BODY) as it:
                for j in range(SEARCH_BODY):
                    def own(ins, k):
                        ins.then_inc(chain, 1)
                        if k:
                            dve.wait_ge(chain, it * (OWN * SEARCH_BODY) + (base + OWN * j + k))
                    own(dve.tensor_tensor(cand[:, :, :].bitcast(u32), over(thr[:, :].bitcast(u32), 3),
                                          steps.unsqueeze(1).to_broadcast([P, E, 3]), ALU.bitwise_or), 1)
                    own(dve.tensor_tensor(passed[:, :, :, :], score[:, :, :].unsqueeze(2).to_broadcast([P, E, 3, G]),
                                          over(cand[:, :, :], G), ALU.is_ge), 2)
                    with nc.allow_low_precision("counts up to 32"):
                        dve.tensor_reduce(passed_n[:, :, :], passed[:, :, :, :], AX.X, ALU.add).then_inc(asked, 1)
                    own(dve.tensor_copy(kept[:, :, 3], thr[:, :]), 0)
                    own(dve.tensor_scalar(steps, steps, 2, None, ALU.logical_shift_right), 0)
                    dve.wait_ge(counted, it * SEARCH_BODY + (j + 1))
                    own(dve.scalar_tensor_tensor(kept[:, :, 0:3], bank[4][:, 0:3 * E].rearrange("p (e j) -> p e j", j=3),
                                                 float(CAP), cand[:, :, :], ALU.is_ge, ALU.mult), 5)
                    own(dve.tensor_reduce(thr[:, :], kept[:, :, :], AX.X, ALU.max), 6)
            n_chain = base + SEARCH_STEPS * OWN

            thr_b = over(thr[:, :], G)
            dve.tensor_tensor(above[:, 0, :, :], score[:, :, :], thr_b, ALU.is_gt)
            dve.tensor_tensor(above[:, 1, :, :], score[:, :, :], thr_b, ALU.is_equal).then_inc(ranks_in, 1)
            dve.wait_ge(ranked, 2)
            flat2 = lambda t: t[:, :, :, :].rearrange("p a e g -> p (a e g)")
            link(dve.tensor_tensor_scan(flat2(incl), restart, bank[6][:, 0:2 * E * G], 0.0, ALU.mult, ALU.add))
            link(dve.tensor_tensor(flat2(prefix), flat2(incl), bank[6][:, 0:2 * E * G], ALU.subtract))
            link(dve.tensor_tensor(flat2(prefix), flat2(prefix), bank[5][:, 0:2 * E * G], ALU.add))
            link(dve.tensor_scalar(need[:, :], incl[:, 0, :, G - 1], -1.0, float(CAP), ALU.mult, ALU.add))
            need_b = over(need[:, :], G)
            link(dve.tensor_tensor(t_eg[0][:, :, :], prefix[:, 1, :, :], need_b, ALU.is_lt))
            link(dve.tensor_tensor(t_eg[0][:, :, :], t_eg[0][:, :, :], above[:, 1, :, :], ALU.mult))
            link(dve.tensor_tensor(t_eg[0][:, :, :], t_eg[0][:, :, :], above[:, 0, :, :], ALU.add))
            link(dve.tensor_tensor(t_eg[1][:, :, :], prefix[:, 1, :, :], need_b, ALU.min))
            link(dve.tensor_tensor(pos_i[0][:, :, :], t_eg[1][:, :, :], prefix[:, 0, :, :], ALU.add))
            link(dve.tensor_scalar(pos_i[1][:, :, :], pos_i[0][:, :, :], 7, None, ALU.logical_shift_right))
            link(dve.tensor_scalar(pos_i[0][:, :, :], pos_i[0][:, :, :], 127, None, ALU.bitwise_and))
            dve.tensor_copy(pos_r[:, :, :], pos_i[0][:, :, :])
            link(dve.tensor_scalar(t_eg[0][:, :, :], t_eg[0][:, :, :], -64.0, 64.0, ALU.mult, ALU.add))
            link(dve.tensor_tensor(pos_q[:, :, :], pos_i[1][:, :, :], t_eg[0][:, :, :], ALU.add))
            dve.wait_ge(vals_in, 1)

            def route_make(e, part, parts=4):
                g = slice(part * G // parts, (part + 1) * G // parts)
                n = G // parts
                link(dve.tensor_tensor(onehot_q[:, g, :], over(pos_q[:, e, g], Q),
                                       iota_b[:, 0:Q].unsqueeze(1).to_broadcast([P, n, Q]), ALU.is_equal))
                dve.tensor_tensor(slotted[:, g, :, :], over(onehot_q[:, g, :], C),
                                  vals[:, e, g, :].unsqueeze(2).to_broadcast([P, n, Q, C]), ALU.mult)
                dve.tensor_tensor(onehot_r[:, g, :], over(pos_r[:, e, g], P),
                                  iota_b[:, :].unsqueeze(1).to_broadcast([P, n, P]), ALU.is_equal).then_inc(route_in, 1)

            def route_read(e):
                dve.wait_ge(route_mm, e + 1)
                link(dve.tensor_copy(routed[:, :, :], bank[7][:, 0:Q * C].rearrange("p (q c) -> p q c", c=C)))
                link(dve.scalar_tensor_tensor(route_t[:, 0, :], routed[:, :, 1], float(P), routed[:, :, 0], ALU.mult, ALU.add))
                link(dve.tensor_scalar(route_t[:, 1, :], routed[:, :, 2], -1.0, 1.0, ALU.mult, ALU.add))
                link(dve.scalar_tensor_tensor(slot_row[:, e, :], route_t[:, 1, :], cols[:, 1:2], route_t[:, 0, :], ALU.mult, ALU.add))
                link(dve.tensor_tensor(route_t[:, 2, :], routed[:, :, 3], routed[:, :, 4], ALU.add))
                dve.tensor_tensor(slot_p[:, e, :], route_t[:, 2, :], routed[:, :, 5], ALU.add).then_inc(route_out, 1)

            for part in range(4):
                route_make(0, part)
            route_read(0)

            def slots_lo(b, k, src):
                dve.wait_ge(xs_hi, KD * b + k + 1)
                hi, lo = xs[b % 2]
                dve.tensor_tensor(lo[:, k, :], src[:, :], hi[:, k, :].bitcast(f32), ALU.subtract).then_inc(xs_lo, 1)

            n_new = 0

            def new_lo(lo, hi, r, done):
                nonlocal n_new
                n_new += 1
                dve.wait_ge(nw_hi, n_new)
                dve.tensor_tensor(lo, r, hi.bitcast(f32), ALU.subtract).then_inc(done, 1)

            for k in range(KD):
                slots_lo(0, k, bank[6 + k])
            for b in range(NB0):
                for h in range(KH):
                    s = KH * b + h
                    hi, lo = hid[s % 4]
                    dve.wait_ge(gelu0, s + 1)
                    if s >= 4:
                        dve.wait_ge(down0, s - 3)
                    dve.tensor_copy(hi[:, :], hf[s % 2][:, :]).then_inc(hi_0, 1)
                    dve.wait_ge(hi_0, s + 1)
                    dve.tensor_tensor(lo[:, :], hf[s % 2][:, :], hi[:, :].bitcast(f32), ALU.subtract).then_inc(hid0, 1)
                    if h in (4, 6) and b + 1 < NB0:
                        slots_lo(b + 1, (4, 6).index(h), bank[6])
                    if b < E - 1 and 1 <= h < 5:
                        if h == 1 and b:
                            dve.wait_ge(route_mm, b + 1)
                        route_make(b + 1, h - 1)
                    if b < E - 1 and h == 7:
                        route_read(b + 1)
                    if b == 0 and h in (0, 5, 6):
                        j = (0, 5, 6).index(h)
                        dve.wait_ge(hi1_late, j + 1)
                        r, (hi_, lo_) = LATE_SPLITS[j]
                        dve.tensor_tensor(lo_[:, :, :], r[:, :, :], hi_[:, :, :].bitcast(f32), ALU.subtract).then_inc(lo1_late, 1)
                    if b % 2 and b < NB0 - 1:
                        hc = slice(h * P, (h + 1) * P)
                        new_lo(w1[1][:, :, hc], w1[0][:, :, hc], w1_raw[:, :, hc], w1_new)
                        if h >= 2:
                            new_lo(w2[1][:, h - 2, :], w2[0][:, h - 2, :], w2_raw[:, h - 2, :], w2_new)
                    if b and b % 2 == 0 and h < 2:
                        new_lo(w2[1][:, KH - 2 + h, :], w2[0][:, KH - 2 + h, :], w2_raw[:, KH - 2 + h, :], w2_new)

            def masked(dst, src, t):
                m = adapter_mask[:, bass.ds(t * SB, SB)]
                return dve.tensor_tensor(dst[:, :].rearrange("p (s n) -> p s n", n=32),
                                         src[:, :].rearrange("p (s n) -> p s n", n=32), over(m, 32), ALU.mult)

            def x1_low(par, n, k, src):
                dve.wait_ge(x1_act, n)
                dve.tensor_tensor(x1s[par][1][:, k, :], src, x1s[par][0][:, k, :].bitcast(f32),
                                  ALU.subtract).then_inc(x1_lo, 1)

            def u_parts(t, j, parts, src):
                n = 2 * t + j + 1
                dve.wait_ge(u_mm, n)
                masked(um[j], src, t).then_inc(u_ev, 1)
                dve.wait_ge(u_ev, n)
                dve.tensor_copy(parts[0][:, :], um[j][:, :]).then_inc(u_hi, 1)
                dve.wait_ge(u_hi, n)
                dve.tensor_tensor(parts[1][:, :], um[j][:, :], parts[0][:, :].bitcast(f32), ALU.subtract).then_inc(u_lo, 1)

            def finish_v(t):
                dve.wait_ge(down1, KH * (t + 1))
                masked(vm, bank[6], t).then_inc(v_ev, 1)
                dve.wait_ge(v_ev, t + 1)
                dve.tensor_copy(vs[0][:, :], vm[:, :]).then_inc(v_hi, 1)
                dve.wait_ge(v_hi, t + 1)
                dve.tensor_tensor(vs[1][:, :], vm[:, :], vs[0][:, :].bitcast(f32), ALU.subtract).then_inc(v_lo, 1)

            def finish_out(t, par, wait_store, halves=False):
                if wait_store is not None:
                    dve.wait_ge(out_done[par], wait_store)
                for k in range(KD):
                    if halves or k == 0:
                        dve.wait_ge(acc1, t + 1 + k)
                    dve.scalar_tensor_tensor(out_sb[par][:, k, :], bank[4 + k][:, :], out_bias[:, k:k + 1],
                                             x1T[par][:, k, :], ALU.add, ALU.add).then_inc(out_ev, 1)

            def steps1(t, par, pair, first, last):
                for h in range(KH):
                    s = KH * t + h
                    if h == 2 and not first:
                        before_ = pair if par else pair - 1
                        prior = None if isinstance(pair, int) and before_ <= 0 else 16 * before_
                        finish_out(t - 1, 1 - par, prior)
                    dve.wait_ge(up1, s + 1)
                    dve.wait_ge(silu1, s + 1)
                    if not (first and h < 2):
                        dve.wait_ge(hid1_s, s - 1)
                    dve.tensor_tensor(prod[h % 2][:, :], bank[2 + h % 2][:, :], act1[h % 2][:, :], ALU.mult).then_inc(prod1, 1)
                    dve.wait_ge(prod1, s + 1)
                    if not (first and h < 4):
                        dve.wait_ge(down1, s - 3)
                    dve.tensor_copy(hid1[h % 4][0][:, :], prod[h % 2][:, :]).then_inc(phi1, 1)
                    dve.wait_ge(phi1, s + 1)
                    dve.tensor_tensor(hid1[h % 4][1][:, :], prod[h % 2][:, :], hid1[h % 4][0][:, :].bitcast(f32),
                                      ALU.subtract).then_inc(hid1_s, 1)
                    if h == 1 and not first:
                        finish_v(t - 1)
                    if h in (3, 4) and not last:
                        x1_low(1 - par, KD * (t + 1) + h - 2, h - 3, x1T[1 - par][:, h - 3, :])
                    if h == 5 and not last:
                        u_parts(t + 1, 0, ug[1 - par], bank[7])
                    if h == 6 and not last:
                        u_parts(t + 1, 1, uu[1 - par], bank[7])

            for k in range(KD):
                x1_low(0, k + 1, k, bank[4 + k][:, :])
            u_parts(0, 0, ug[0], bank[7])
            u_parts(0, 1, uu[0], bank[6])
            steps1(0, 0, 0, True, False)
            steps1(1, 1, 0, False, False)
            with dve.Fori(1, NB1 // 2 - 1) as i:
                steps1(2 * i, 0, i, False, False)
                steps1(2 * i + 1, 1, i, False, False)
            steps1(NB1 - 2, 0, NB1 // 2 - 1, False, False)
            steps1(NB1 - 1, 1, NB1 // 2 - 1, False, True)
            finish_v(NB1 - 1)
            finish_out(NB1 - 1, 1, 16 * (NB1 // 2 - 1), halves=True)

        @block.tensor
        def _(pe):
            def product(out, lhs, rhs, start, stop):
                (lh, ll), (rh, rl) = lhs, rhs
                pe.matmul(out, lh, rh, start=start, stop=False, skip_group_check=True)
                pe.matmul(out, lh, rl, start=False, stop=False, skip_group_check=True)
                return pe.matmul(out, ll, rh, start=False, stop=stop, skip_group_check=True)

            def at(parts, *index):
                return tuple(p[index] for p in parts)

            every = slice(None)
            pe.wait_ge(pack_in, 32)

            def z_by_token(h):
                pe.wait_ge(z_ev, h + 1)
                if h:
                    pe.wait_ge(z_in, 1)
                for c in range(GB):
                    last = pe.transpose(bank[3][:, c * P:(c + 1) * P], zT[:, c * P:(c + 1) * P], ident)
                last.then_inc(z_tr, 1)

            def logits(h):
                pe.wait_ge(z_in, h + 1)
                for c in range(4):
                    for j in range(4):
                        g = h * 16 + j * 4 + c
                        last = pe.matmul(bank[5 + h][32 * j:32 * j + 32, c * P:(c + 1) * P], z[:, g, :], mix[:, g, :],
                                         start=True, stop=True, tile_position=(0, 32 * j))
                last.then_inc(logit_mm, 1)

            def logits_by_token(h):
                pe.wait_ge(logit_ev, h + 1)
                if h:
                    pe.wait_ge(z_ev, 2)
                for c in range(4):
                    last = pe.transpose(bank[4 + 3 * h][:, c * P:(c + 1) * P], logitT[:, h, c * P:(c + 1) * P], ident)
                last.then_inc(logit_tr, 1)

            for i in range(8):
                pe.wait_ge(xT_in[i], 16)
                j = i % 4
                for k in range(KD):
                    last = pe.matmul(bank[2 + 5 * (i // 4)][32 * j:32 * j + 32, :], gate_w[:, k, :], xT[i][:, k, :],
                                     start=k == 0, stop=k == KD - 1, tile_position=(0, 32 * j))
                if j == 3:
                    last.then_inc(z_mm, 1)
                if i == 5:
                    z_by_token(0)
            z_by_token(1)
            pe.wait_ge(mixed, 4)
            logits(0)
            logits(1)
            logits_by_token(0)
            logits_by_token(1)

            def item(n):
                if n == 0:
                    pe.wait_ge(z_in, 2)
                if n >= 4:
                    pe.wait_ge(item_ev, n - 3)
                out = bank[n % 4]
                if n < G:
                    if n % GB == 0:
                        pe.wait_ge(x_in[n // GB], 16)
                    last = pe.matmul(out[:, 0:D], mix[:, n, :], x_sb[:, n, :], start=True, stop=True)
                elif n < ITEMS - 1:
                    if n == G:
                        pe.wait_ge(fold_in, 1)
                    for a in range(2):
                        h = 2 * (n - G) + a
                        for k in range(KD):
                            last = pe.matmul(out[:, a * D:(a + 1) * D], wdT[:, k, h * P:(h + 1) * P], wfT_s[:, k, :],
                                             start=k == 0, stop=k == KD - 1)
                else:
                    for k in range(KD):
                        last = pe.matmul(out[:, 0:D], bdT[:, k, :], wfT_s[:, k, :], start=k == 0, stop=k == KD - 1)
                last.then_inc(item_mm, 1)

            for n in range(ROWS_FIRST):
                item(n)
            n = ROWS_FIRST
            for i in range(SEARCH_STEPS):
                pe.wait_ge(asked, i + 1)
                pe.matmul(bank[4][:, 0:3 * E], ones_b[:, :], passed_n[:, :, :].rearrange("p e j -> p (e j)"),
                          start=True, stop=True).then_inc(counted, 1)
                for _ in range(2 if i < 6 else 3 if n < G else 1):
                    if n < ITEMS:
                        item(n)
                        n += 1
            assert n == ITEMS
            pe.wait_ge(ranks_in, 1)
            marks = above[:, :, :, :].rearrange("p a e g -> p (a e g)")
            pe.matmul(bank[5][:, 0:2 * E * G], before_b[:, :], marks, start=True, stop=True).then_inc(ranked, 1)
            pe.matmul(bank[6][:, 0:2 * E * G], ones_b[:, :], marks, start=True, stop=True).then_inc(ranked, 1)

            def keep_busy(n, into, parts):
                for _ in range(n):
                    pe.matmul(into[:, :], parts[0][:, 0, 0:P], parts[0][:, 0, 0:BT], start=True, stop=True)

            def route(e):
                if e:
                    pe.wait_ge(route_out, e)
                for g in range(G):
                    if g % (G // 4) == 0:
                        pe.wait_ge(route_in, 4 * e + g // (G // 4) + 1)
                    last = pe.matmul(bank[7][:, 0:Q * C], onehot_r[:, g, :], slotted[:, g, :, :].rearrange("p q c -> p (q c)"),
                                     start=g == 0, stop=g == G - 1)
                last.then_inc(route_mm, 1)

            def slots_transposed(b, k, into):
                if b:
                    pe.wait_ge(xs_lo, KD * b + k)
                for c in range(GB):
                    if b == 0 and k == 0 and c:
                        keep_busy(WAIT_ROWS, bank[2], w1)
                    pe.wait_ge(gathered[c], 16 * (b + 1))
                    last = pe.transpose(into[:, c * P:(c + 1) * P].bitcast(f32r), xg[:, c, k * P:(k + 1) * P].bitcast(f32r), ident_r[:, :])
                last.then_inc(xsT, 1)

            route(0)
            pe.wait_ge(ident_in, 1)
            pe.wait_ge(lo0, 4)
            pe.wait_ge(item_ev, ITEMS)
            keep_busy(WAIT_GATHER, bank[2], w1)
            for k in range(KD):
                slots_transposed(0, k, bank[6 + k])
            keep_busy(WAIT_PARTS0, bank[2], w1)

            def down(s):
                b, h = s // KH, s % KH
                pe.wait_ge(hid0, s + 1)
                if h == 0 and b >= 2:
                    pe.wait_ge(y_out, GB * (b - 1))
                if b % 2 == 0 and b:
                    pe.wait_ge(w2_new, KH * (b // 2 - 1) + h + 1)
                for q in range(GB):
                    out = y_at(b, q)
                    last = product(out, at(hid[s % 4], every, slice(q * P, (q + 1) * P)), at(w2, every, h, every),
                                   start=h == 0 and (q % 2 == 0 or b == NB0 - 1), stop=h == KH - 1)
                last.then_inc(down0, 1)

            for b in range(NB0):
                for h in range(KH):
                    s = KH * b + h
                    if s >= 2:
                        pe.wait_ge(gelu0, s - 1)
                    if h == 0:
                        pe.wait_ge(xs_lo, KD * (b + 1))
                    if b % 2 == 0 and b:
                        pe.wait_ge(w1_new, KH * (b // 2 - 1) + h + 1)
                    for k in range(KD):
                        last = product(bank[s % 2][:, :], at(w1, every, k, slice(h * P, (h + 1) * P)),
                                       at(xs[b % 2], every, k, every), start=k == 0, stop=k == KD - 1)
                    last.then_inc(up0, 1)
                    if 2 <= s < KH * NB0 - 2:
                        down(s - 2)
                    if h in (3, 5) and b + 1 < NB0:
                        slots_transposed(b + 1, (3, 5).index(h), bank[6])
                    if h == 6 and b < E - 1:
                        route(b + 1)
            def down_quarter(s, q):
                pe.wait_ge(hid0, s + 1)
                return product(y_at(NB0 - 1, q), at(hid[s % 4], every, slice(q * P, (q + 1) * P)), at(w2, every, s % KH, every),
                               start=False, stop=s == KH * NB0 - 1)

            end = KH * NB0
            for q in range(2):
                for s in range(end - 4, end - 1):
                    down_quarter(s, q)
            for q in range(GB):
                for s in range(end - 4 if q >= 2 else end - 1, end):
                    last = down_quarter(s, q)
                last.then_inc(down0, 1)

            def x1_transposed(par, loads, prior, k, into):
                pe.wait_ge(x1_in[par], loads)
                if prior is not None:
                    pe.wait_ge(*prior)
                for c in range(GB):
                    last = pe.transpose(into[:, c * P:(c + 1) * P].bitcast(f32r), x1_sb[par][:, c, k * P:(k + 1) * P].bitcast(f32r), ident_r[:, :])
                last.then_inc(x1_t, 1)

            def low_rank(par, w, into):
                for k in range(KD):
                    last = product(into[:, :], at(w, every, k, every), at(x1s[par], every, k, every),
                                   start=k == 0, stop=k == KD - 1)
                last.then_inc(u_mm, 1)

            def prepare(t, par, pair, h):
                if h == 3:
                    x1_transposed(par, 16 * (pair + 1), (u_ev, 2 * t), 0, bank[7])
                if h == 4:
                    x1_transposed(par, 16 * (pair + 1), (x1_act, KD * t + 1), 1, bank[7])
                if h == 5:
                    pe.wait_ge(x1_lo, KD * (t + 1))
                    low_rank(par, ag, bank[7])
                if h == 6:
                    pe.wait_ge(u_ev, 2 * t + 1)
                    low_rank(par, au, bank[7])

            def half(w, b, u, x, out, h, done, u_parts_done):
                hc = slice(h * P, (h + 1) * P)
                for k in range(KD):
                    product(out, at(w, every, k, hc), at(x, every, k, every), start=k == 0, stop=False)
                if h == 0:
                    pe.wait_ge(u_lo, u_parts_done)
                product(out, at(b, every, 0, hc), at(u, every, every), start=False, stop=True).then_inc(done, 1)

            def down1_(s, h, t, first, low_rank_first=False):
                pe.wait_ge(hid1_s, s + 1)
                if h == 0 and not first:
                    pe.wait_ge(out_ev, KD * t)
                if low_rank_first:
                    product(bank[6][:, :], at(ad, every, h, every), at(hid1[h % 4], every, every),
                            start=False, stop=True).then_inc(down1, 1)
                for k in range(KD):
                    product(bank[4 + k][:, :], at(wd, every, h, slice(k * P, (k + 1) * P)), at(hid1[h % 4], every, every),
                            start=h == 0, stop=False)
                if not low_rank_first:
                    product(bank[6][:, :], at(ad, every, h, every), at(hid1[h % 4], every, every),
                            start=h == 0, stop=h == KH - 1).then_inc(down1, 1)

            def finish(t, halves=False):
                pe.wait_ge(v_lo, t + 1)
                for k in range(KD):
                    last = product(bank[4 + k][:, :], at(bd, every, 0, slice(k * P, (k + 1) * P)), at(vs, every, every),
                                   start=False, stop=True)
                    if halves or k == KD - 1:
                        last.then_inc(acc1, 1)

            def steps1(t, par, pair, first, last):
                for h in range(KH):
                    s = KH * t + h
                    if not (first and h < 2):
                        pe.wait_ge(silu1, s - 1)
                        pe.wait_ge(prod1, s - 1)
                    half(wg, bg, ug[par], x1s[par], bank[h % 2][:, :], h, gate1, 2 * t + 1)
                    if h == 2 and not first:
                        finish(t - 1)
                    half(wu, bu, uu[par], x1s[par], bank[2 + h % 2][:, :], h, up1, 2 * t + 2)
                    if h >= 2:
                        down1_(s - 2, h - 2, t, first)
                    elif not first:
                        down1_(s - 2, KH - 2 + h, t - 1, False)
                    if not last:
                        prepare(t + 1, 1 - par, pair + par, h)

            pe.wait_ge(lo1, NP1)
            pe.wait_ge(lo1_late, 3)
            keep_busy(WAIT_X1, bank[0], wg)
            for k in range(KD):
                x1_transposed(0, 16, None, k, bank[4 + k])
            for k in range(KD):
                pe.wait_ge(x1_lo, k + 1)
                last = product(bank[7][:, :], at(ag, every, k, every), at(x1s[0], every, k, every),
                               start=k == 0, stop=k == KD - 1)
            last.then_inc(u_mm, 1)
            low_rank(0, au, bank[6])
            steps1(0, 0, 0, True, False)
            steps1(1, 1, 0, False, False)
            with pe.Fori(1, NB1 // 2 - 1) as i:
                steps1(2 * i, 0, i, False, False)
                steps1(2 * i + 1, 1, i, False, False)
            steps1(NB1 - 2, 0, NB1 // 2 - 1, False, False)
            steps1(NB1 - 1, 1, NB1 // 2 - 1, False, True)
            down1_(KH * NB1 - 2, KH - 2, NB1 - 1, False)
            down1_(KH * NB1 - 1, KH - 1, NB1 - 1, False, low_rank_first=True)
            finish(NB1 - 1, halves=True)


def kernel(**inputs):
    import concourse.bacc as _bacc
    from concourse import mybir as _mybir
    from concourse.bass_utils import run_bass_kernel_spmd as _run

    a = {k: np.asarray(v) for k, v in inputs.items()}
    consts = shape_constants()
    itok = a["itok_B_0_7"]
    wide = lambda v: np.broadcast_to(v, (P, v.size))
    gate_w = np.zeros((P, KD, 32), a["L0_ffn_Wg"].dtype)
    gate_w[:, :, :E] = a["L0_ffn_Wg"].reshape(KD, P, E).transpose(1, 0, 2)
    small = {
        **consts,
        "gate_w": gate_w.reshape(P, KD * 32),
        "subj_w": np.tile(a["L0_cond_weights"].transpose(1, 0, 2).reshape(32, NAD * 32), (4, 1)),
        "subj": np.repeat(itok.reshape(G, 4).T, 32, axis=0),
        "sample": wide(itok), "gate_b": wide(a["L0_ffn_bg"]), "scale": wide(a["L1_ffn_scale_weight"]),
        "out_bias": a["L1_ffn_bias"].reshape(KD, P).T,
    }
    arrays = {
        **{n: np.concatenate([small[c] for c in names], 1)
           for n, names in (("pack_f", F_COLS), ("pack_f2", F2_COLS), ("pack_i", I_COLS))},
        "x": a["x"].reshape(TOK, D),
        "xT": a["x"].reshape(TOK, D).T,
        "L0_ffn_W1": a["L0_ffn_W1"], "L0_ffn_W2": a["L0_ffn_W2"],
        "L1_cond_Wg": a["L1_cond_Wg"], "L1_cond_Wu": a["L1_cond_Wu"],
        "wdT": a["L1_cond_Wd"].T,
        "ag_all": a["L1_cond_Ag"].transpose(1, 0, 2).reshape(D, P),
        "au_all": a["L1_cond_Au"].transpose(1, 0, 2).reshape(D, P),
        "ad_all": a["L1_cond_Ad"].transpose(1, 0, 2).reshape(HID, P),
        "bg_all": a["L1_cond_Bg"].reshape(P, HID),
        "bu_all": a["L1_cond_Bu"].reshape(P, HID),
        "bdT": a["L1_cond_Bd"].reshape(P, D).T,
        "wfT": a["L1_ffn_weight"].T,
    }
    arrays = {f"in_{n}": np.ascontiguousarray(v) for n, v in arrays.items()}
    nc = _bacc.Bacc("TRN2", target_bir_lowering=False, num_devices=1)
    args = {n[3:]: nc.dram_tensor(n, v.shape, _mybir.dt.from_np(v.dtype), kind="ExternalInput").ap()
            for n, v in arrays.items()}
    outT = nc.dram_tensor("outT", (KD, P, TOK), _mybir.dt.float32, kind="ExternalOutput").ap()
    adaln_moe_lora(nc, args, outT)
    r = _run(nc, [arrays], core_ids=[0])
    got = r.results[0]["outT"].reshape(D, TOK)
    return np.ascontiguousarray(got.T).reshape(a["x"].shape)
```
